# Optimizing a Trainium2 kernel written in Bass

```python
import numpy as np
import jax
import jax.numpy as jnp

def _softmax(x, axis=-1):
    return jax.nn.softmax(x, axis=axis)

def _gelu(x):
    return jax.nn.gelu(x, approximate=True)

def _silu(x):
    return jax.nn.silu(x)

def _sigmoid(x):
    return jax.nn.sigmoid(x)

def _layernorm(x, axis=-1, eps=1e-05):
    m = jnp.mean(x, axis=axis, keepdims=True)
    v = jnp.var(x, axis=axis, keepdims=True)
    return (x - m) / jnp.sqrt(v + eps)

def _scatter_add(tgt, idx, src, axis=0):
    return tgt.at[idx].add(src)

def _segment_sum(src, seg, n):
    return jax.ops.segment_sum(src, seg, n)
kernel_name = 'mk_adj_ffn_d1_adj_r2_96b6dd'

def setup_inputs(seed: int=0):
    np.random.seed(seed)
    _w = jnp.asarray

    def _rec_inputs():
        import jax
        import jax.numpy as jnp
        _gk = jax.random.key(seed)
        x = -1.394e-06 + 0.9999 * jax.random.normal(jax.random.fold_in(_gk, 1), (32, 256, 256), jnp.float32)
        _w = (1.0 + jnp.arange(256, dtype=jnp.float32)) ** (-0.5)
        _w = _w / _w.mean()
        _pij = jnp.clip(0.0078125 * _w[:, None] * _w[None, :], 0.0, 1.0)
        _a = jax.random.uniform(jax.random.fold_in(_gk, 2), (32, 256, 256)) < _pij
        adj = _a.astype(jnp.int32)
        return (x, adj)
    x, adj = _rec_inputs()

    def _L0_gnn_setup():
        import jax, jax.numpy as jnp
        import numpy as np
        NEG_INF = -1000000000.0
        NEG_SLOPE = 0.2

        def gat_layer(x, mask, W, a_src, a_dst, bias, concat):
            B, N, _ = x.shape
            H, F = a_src.shape
            xl = (x @ W).reshape(B, N, H, F)
            asrc = jnp.einsum('bnhf,hf->bnh', xl, a_src)
            adst = jnp.einsum('bnhf,hf->bnh', xl, a_dst)
            e = jax.nn.leaky_relu(asrc[:, :, None, :] + adst[:, None, :, :], NEG_SLOPE)
            e = jnp.where(mask[..., None], e, NEG_INF)
            attn = jax.nn.softmax(e, axis=1)
            out = jnp.einsum('bsdh,bshf->bdhf', attn, xl)
            if concat:
                out = out.reshape(B, N, H * F)
            else:
                out = out.mean(axis=2)
            return out + bias
        key = jax.random.key(seed)
        ks = jax.random.split(key, 10)
        B, N, Din, Fh, H, Dout = (8, 512, 256, 128, 4, 256)
        s = 0.05
        return {'adj': jax.random.randint(ks[0], (B, N, N), 0, 2, dtype=jnp.int32), 'x': jax.random.normal(ks[1], (B, N, Din), dtype=jnp.float32), 'W1': jax.random.normal(ks[2], (Din, H * Fh), dtype=jnp.float32) * s, 'att_src1': jax.random.normal(ks[3], (H, Fh), dtype=jnp.float32) * s, 'att_dst1': jax.random.normal(ks[4], (H, Fh), dtype=jnp.float32) * s, 'b1': jax.random.normal(ks[5], (H * Fh,), dtype=jnp.float32) * s, 'W2': jax.random.normal(ks[6], (H * Fh, Dout), dtype=jnp.float32) * s, 'att_src2': jax.random.normal(ks[7], (1, Dout), dtype=jnp.float32) * s, 'att_dst2': jax.random.normal(ks[8], (1, Dout), dtype=jnp.float32) * s, 'b2': jax.random.normal(ks[9], (Dout,), dtype=jnp.float32) * s}
    _L0_gnn_all = _L0_gnn_setup()
    _L0_gnn_in = {k: v for k, v in _L0_gnn_all.items() if k in ('W1', 'att_src1', 'att_dst1', 'b1', 'W2', 'att_src2', 'att_dst2', 'b2')}
    del _L0_gnn_all

    def _L0_ffn_setup():
        import jax, jax.numpy as jnp
        import numpy as np
        TOP_K = 2
        key = jax.random.key(seed)
        k0, k1, k2, k3, k4 = jax.random.split(key, 5)
        B, S, D, F, E = (1, 1024, 256, 512, 8)
        scale = 0.02
        hidden_states = jax.random.normal(k0, (B, S, D), dtype=jnp.float32)
        router_w = jax.random.normal(k1, (D, E), dtype=jnp.float32) * scale
        w1 = jax.random.normal(k2, (E, D, F), dtype=jnp.float32) * scale
        w2 = jax.random.normal(k3, (E, F, D), dtype=jnp.float32) * scale
        w3 = jax.random.normal(k4, (E, D, F), dtype=jnp.float32) * scale
        return {'hidden_states': hidden_states, 'router_w': router_w, 'w1': w1, 'w2': w2, 'w3': w3}
    _L0_ffn_all = _L0_ffn_setup()
    _L0_ffn_in = {k: v for k, v in _L0_ffn_all.items() if k in ('router_w', 'w1', 'w2', 'w3')}
    del _L0_ffn_all
    return {'x': x, 'adj': adj, 'L0_gnn_W1': _L0_gnn_in['W1'], 'L0_gnn_att_src1': _L0_gnn_in['att_src1'], 'L0_gnn_att_dst1': _L0_gnn_in['att_dst1'], 'L0_gnn_b1': _L0_gnn_in['b1'], 'L0_gnn_W2': _L0_gnn_in['W2'], 'L0_gnn_att_src2': _L0_gnn_in['att_src2'], 'L0_gnn_att_dst2': _L0_gnn_in['att_dst2'], 'L0_gnn_b2': _L0_gnn_in['b2'], 'L0_ffn_router_w': _L0_ffn_in['router_w'], 'L0_ffn_w1': _L0_ffn_in['w1'], 'L0_ffn_w2': _L0_ffn_in['w2'], 'L0_ffn_w3': _L0_ffn_in['w3']}

def reference(x, adj, L0_gnn_W1, L0_gnn_att_src1, L0_gnn_att_dst1, L0_gnn_b1, L0_gnn_W2, L0_gnn_att_src2, L0_gnn_att_dst2, L0_gnn_b2, L0_ffn_router_w, L0_ffn_w1, L0_ffn_w2, L0_ffn_w3):
    import jax
    import jax.numpy as jnp

    def _L0_gnn_ref(adj, x, W1, att_src1, att_dst1, b1, W2, att_src2, att_dst2, b2):
        import jax, jax.numpy as jnp
        import numpy as np
        NEG_INF = -1000000000.0
        NEG_SLOPE = 0.2

        def gat_layer(x, mask, W, a_src, a_dst, bias, concat):
            B, N, _ = x.shape
            H, F = a_src.shape
            xl = (x @ W).reshape(B, N, H, F)
            asrc = jnp.einsum('bnhf,hf->bnh', xl, a_src)
            adst = jnp.einsum('bnhf,hf->bnh', xl, a_dst)
            e = jax.nn.leaky_relu(asrc[:, :, None, :] + adst[:, None, :, :], NEG_SLOPE)
            e = jnp.where(mask[..., None], e, NEG_INF)
            attn = jax.nn.softmax(e, axis=1)
            out = jnp.einsum('bsdh,bshf->bdhf', attn, xl)
            if concat:
                out = out.reshape(B, N, H * F)
            else:
                out = out.mean(axis=2)
            return out + bias
        B, N, _ = adj.shape
        mask = (adj > 0) | jnp.eye(N, dtype=bool)[None]
        h = jax.nn.elu(gat_layer(x, mask, W1, att_src1, att_dst1, b1, concat=True))
        h = gat_layer(h, mask, W2, att_src2, att_dst2, b2, concat=False)
        return h

    def _L0_ffn_ref(hidden_states, router_w, w1, w2, w3):
        import jax, jax.numpy as jnp
        import numpy as np
        TOP_K = 2
        B, S, D = hidden_states.shape
        E = router_w.shape[1]
        x = hidden_states.reshape(-1, D)
        T = x.shape[0]
        router_logits = x @ router_w
        probs = jax.nn.softmax(router_logits.astype(jnp.float32), axis=-1)
        routing_weights, selected_experts = jax.lax.top_k(probs, TOP_K)
        routing_weights = routing_weights / routing_weights.sum(axis=-1, keepdims=True)
        routing_weights = routing_weights.astype(x.dtype)
        combine = jnp.zeros((T, E), dtype=x.dtype).at[jnp.arange(T)[:, None], selected_experts].add(routing_weights)
        gate = jax.nn.silu(jnp.einsum('td,edf->tef', x, w1))
        up = jnp.einsum('td,edf->tef', x, w3)
        h = gate * up * combine[:, :, None]
        out = jnp.einsum('tef,efd->td', h, w2)
        return out.reshape(B, S, D)
    x = x + _L0_gnn_ref(adj, _layernorm(x, axis=-1), L0_gnn_W1, L0_gnn_att_src1, L0_gnn_att_dst1, L0_gnn_b1, L0_gnn_W2, L0_gnn_att_src2, L0_gnn_att_dst2, L0_gnn_b2)
    x = x + _L0_ffn_ref(_layernorm(x, axis=-1), L0_ffn_router_w, L0_ffn_w1, L0_ffn_w2, L0_ffn_w3)
    return x

_drawn_inputs = setup_inputs


def setup_inputs(seed=0):
    import zlib

    import numpy as np

    out = dict(_drawn_inputs(seed))
    spreads = {}
    factors = {'L0_gnn_att_dst1': 3.278,
     'L0_gnn_att_dst2': 4.782,
     'L0_ffn_router_w': 4.259,
     'L0_ffn_w1': 3.715,
     'L0_ffn_w2': 3.672,
     'L0_ffn_w3': 3.677}
    for name, (base, spread) in spreads.items():
        noise = np.random.default_rng([zlib.crc32(name.encode()), seed]).standard_normal(out[name].shape)
        drawn = base * np.exp(spread * noise) if base else spread * noise
        out[name] = jnp.asarray(drawn.astype(out[name].dtype))
    for name, factor in factors.items():
        out[name] = (out[name] * factor).astype(out[name].dtype)
    return out
```

```python
from contextlib import ExitStack

import concourse.bass as bass
from concourse import mybir

ALU = mybir.AluOpType
ACT = mybir.ActivationFunctionType
F32 = mybir.dt.float32
F32R = mybir.dt.float32r
BF16 = mybir.dt.bfloat16
I32 = mybir.dt.int32
U32 = mybir.dt.uint32
AX_X = mybir.AxisListType.X

P = 128
NEG_SLOPE = 0.2
LN_EPS = 1e-5
MASKED = 1e30
LOWEST = -3.0e38
RSQRT_SEED = 1597463007.0
NEWTON_STEPS = 3


def gat_moe_kernel(nc, x, adj, W1, a_src1, a_dst1, b1, W2, a_src2, a_dst2, b2, router_w, w1, w2, w3, out):
    B, N, D = x.shape
    H, FH = a_src1.shape
    HF = H * FH
    E, _, F = w1.shape
    NJ = N // P
    KD = D // P
    KF = HF // P
    FT = F // P
    BLK = 512
    SB_B = 4
    SB_T = SB_B * N
    NBLK = SB_T // BLK
    TT = BLK // P
    NSB = B // SB_B
    EI = E // SB_B
    UNITS = EI * NBLK * FT
    WC = KD * F
    W2N = D + 2
    assert N == 256 and D == 256 and FH == P and WC == FT * D == 1024 and NSB % 2 == 0

    with ExitStack() as ctx:
        def sb(name, shape, dt):
            return ctx.enter_context(nc.sbuf_tensor(name, shape, dt))

        def sem(name):
            return ctx.enter_context(nc.semaphore(name))

        ident = sb("ident", [P, P], F32)
        ident_r = sb("ident_r", [P, P], F32R)
        ident_b = sb("ident_b", [P, P], BF16)
        eye = sb("eye", [P, NJ, N], BF16)
        head_row = sb("head_row", [2 * H, H, P], F32R)
        expert_id = sb("expert_id", [P, E], F32)
        W1s = [sb(f"W1_{s}", [P, KD, HF], F32R) for s in "hl"]
        W2s = [sb(f"W2_{s}", [P, KF, W2N], F32R) for s in "hl"]
        v1s = [sb(f"v1_{s}", [P, KD, P], F32R) for s in "hl"]
        rws = [sb(f"rw_{s}", [P, KD, P], F32R) for s in "hl"]
        v2f = sb("v2f", [P, KF, 2], F32)
        b1T = sb("b1T", [P, H], F32)
        b2b = sb("b2b", [P, D], F32)

        stage = sb("stage", [P, 2, WC], F32)
        we1 = [[sb(f"we1_{e}{s}", [P, KD, F], F32R) for s in "hl"] for e in range(EI)]
        we3 = [[sb(f"we3_{e}{s}", [P, KD, F], F32R) for s in "hl"] for e in range(EI)]
        we2 = [[sb(f"we2_{e}{s}", [P, FT, D], F32R) for s in "hl"] for e in range(EI)]

        xTs = [sb(f"xT_{s}", [P, KD, 2 * SB_T], F32R) for s in "hl"]
        yacc = sb("yacc", [P, 2 * SB_B * NJ, D], F32)
        comb = sb("comb", [P, 2 * SB_B * NJ, E], F32)
        cw = sb("cw", [P, SB_B * NJ, EI], F32)
        hb = sb("hb", [P, 2, BLK], F32)
        hhs = [sb(f"hh_{s}", [P, 2, BLK], F32R) for s in "hl"]

        xb = sb("xb", [P, NJ, D], F32)
        adjb = sb("adjb", [P, NJ, N], I32)
        xn = sb("xn", [P, NJ, D], F32)
        mask = sb("mask", [P, NJ, N], BF16)
        mbias = sb("mbias", [P, NJ, N], F32)
        nTs = [sb(f"nT_{s}", [P, KD, N], F32R) for s in "hl"]
        rows_f = sb("rows_f", [2 * H, N], F32)
        rows_s = [sb(f"rows_{s}", [2 * H, N], F32R) for s in "hl"]
        lrows = sb("lrows", [E, N], F32)
        cols = sb("cols", [P, NJ, 2 * H], F32)
        xls = [sb(f"xl_{s}", [P, NJ, HF], F32R) for s in "hl"]
        sc = sb("sc", [P, 2, NJ, N], F32)
        e1 = sb("e1", [P, 2, NJ, N], F32)
        e2 = sb("e2", [P, 2, NJ, N], F32)
        PTs = [sb(f"PT_{s}", [P, 2, NJ, N], F32R) for s in "hl"]
        z = sb("z", [P, H, N], F32)
        t = sb("t", [P, H, N], F32)
        h1s = [sb(f"h1_{s}", [P, KF, N], F32R) for s in "hl"]
        a2c = sb("a2c", [P, NJ, 2], F32)
        a2s = [sb(f"a2_{s}", [P, NJ, P], F32R) for s in "hl"]
        st = sb("st", [P, NJ, 6], F32)
        mv = sb("mv", [P, NJ, 2], F32)
        nw = sb("nw", [P, 4, NJ], F32)
        mx = sb("mx", [P, NJ, 2], F32)
        mm_ = sb("mm_", [P, NJ, 2], F32)
        bi1 = sb("bi1", [P, NJ, 2], F32)
        bi2 = sb("bi2", [P, NJ, 2], F32)
        sm = sb("sm", [P, NJ, 2], F32)
        rs = sb("rs", [P, NJ, 2], F32)
        lg = sb("lg", [P, NJ, E], F32)
        top = sb("top", [P, NJ, 8], F32)
        topi = sb("topi", [P, NJ, 8], U32)
        topf = sb("topf", [P, NJ, 8], F32)
        gap = sb("gap", [P, NJ], F32)
        eg = sb("eg", [P, NJ], F32)
        wts = sb("wts", [P, 3, NJ], F32)
        oh = sb("oh", [P, 2, NJ, E], F32)

        pG = [ctx.enter_context(nc.psum_tensor(f"pG{i}", [P, BLK], F32)) for i in range(2)]
        pU = [ctx.enter_context(nc.psum_tensor(f"pU{i}", [P, BLK], F32)) for i in range(2)]
        pY = [ctx.enter_context(nc.psum_tensor(f"pY{i}", [P, 2, D], F32)) for i in range(2)]
        pA = ctx.enter_context(nc.psum_tensor("pA", [P, 512], F32))
        pB = ctx.enter_context(nc.psum_tensor("pB", [P, 512], F32))

        maskT = pB[:, 0:NJ * N // 2].bitcast(BF16)
        bank_PT = [pA, pB, pB, pA, pB]
        bank_A1 = [pA, pB]
        bank_X2 = [pA, pB]

        def flat(t_):
            return t_[:, :, :].rearrange("p a b -> p (a b)")

        def fold(t_, n=2):
            return t_[:, :].rearrange("p (a b) -> p a b", a=n)

        s_cin = sem("const_loaded")
        s_w12 = sem("gat_weights_loaded")
        s_cz = sem("const_zeroed")
        s_cid = sem("const_built")
        s_cr = sem("const_rounded")
        s_prep = sem("prep_order")
        s_prepd = sem("prep_done")
        s_x = sem("x_loaded")
        s_adj = sem("adj_loaded")
        s_xb2 = sem("bias2_added")
        s_maskp = sem("mask_marks_2_per_graph")
        s_mask = sem("mask_ready")
        s_dg = sem("dve_graph_order")
        s_ln1 = sem("ln1_ready")
        s_T1 = sem("T1_done")
        s_nTh = sem("nT_high")
        s_nT = sem("nT_ready")
        s_MT = sem("mask_transposed")
        s_mb = sem("mask_bias_ready")
        s_RW = sem("score_rows_done")
        s_rwc = sem("score_rows_copied")
        s_rwl = sem("score_rows_low")
        s_CT = sem("score_cols_done")
        s_cols = sem("score_cols_copied")
        s_X1 = sem("features1_done_2_per_graph")
        s_xlh = sem("features1_high_2_per_graph")
        s_xll = sem("features1_low_2_per_graph")
        s_SB = sem("source_scores_spread_2_per_graph")
        s_max = sem("score_bias_ready_3_per_graph")
        s_exp = sem("exps_done_3_per_graph")
        s_pn = sem("probs_ready_3_per_graph")
        s_PT = sem("probs_transposed_5_per_graph")
        s_PTh = sem("probsT_high_5_per_graph")
        s_PTl = sem("probsT_low_5_per_graph")
        s_A1 = sem("attended1_done_4_per_graph")
        s_z = sem("attended1_biased_2_per_graph")
        s_zn = sem("elu_negative_part_2_per_graph")
        s_ze = sem("elu_exp_2_per_graph")
        s_zf = sem("elu_done_2_per_graph")
        s_h1h = sem("h1_high_2_per_graph")
        s_h1 = sem("h1_ready_2_per_graph")
        s_X2 = sem("features2_done_2_per_graph")
        s_x2h = sem("features2_high_2_per_graph")
        s_x2l = sem("features2_low_2_per_graph")
        s_a2 = sem("source2_columns_ready")
        s_B2 = sem("source2_scores_spread")
        s_A2 = sem("attended2_done")
        s_x1 = sem("gnn_residual_ready")
        s_ln2 = sem("ln2_ready")
        s_T2 = sem("T2_done")
        s_fTh = sem("ffn_xT_high")
        s_fT = sem("ffn_xT_ready")
        s_RT = sem("router_rows_done")
        s_lr = sem("router_rows_copied")
        s_LC = sem("router_cols_done")
        s_lg = sem("router_cols_copied")
        s_gap = sem("logit_gap_ready")
        s_eg = sem("gap_exp_done")
        s_comb = sem("combine_ready")
        s_res = sem("residual_in_yacc")
        s_wst = [sem("chunk_loaded_0"), sem("chunk_loaded_1")]
        s_wh = sem("chunk_high")
        s_wl = sem("chunk_split")
        s_g = sem("gate_done")
        s_u = sem("up_done")
        s_th = sem("tanh_done")
        s_a = sem("gate_used")
        s_h = sem("hidden_ready")
        s_hh = sem("hidden_high")
        s_hl = sem("hidden_low")
        s_dn = sem("down_done")
        s_cw = sem("weights_of_pair_ready")
        s_y = sem("y_added")
        s_out = sem("out_stored")

        CREDIT = 2
        LAG = 2
        GROUPS = EI * NBLK
        DVE_LINKS = 57
        NW = 3
        NWI = NW * EI

        block = ctx.enter_context(nc.Block())

        def run_iterations(eng, graph_only, ffn):
            with eng.Fori(0, SB_B) as p:
                graph_only(p, p, 0)
            with eng.Fori(0, NSB // 2 - 1) as s2:
                for par in range(2):
                    with eng.Fori(0, SB_B) as p:
                        ffn(s2 * (2 * SB_B) + SB_B * par, p, par)
            with eng.Fori(0, SB_B) as p:
                ffn(B - 2 * SB_B, p, 0)
            with eng.Fori(0, SB_B - 1) as p:
                ffn(B - SB_B, p, 1, graph=False)
            ffn(B - SB_B, SB_B - 1, 1, graph=False, last=True)

        def wait_alone(eng, *waits):
            counts = [(s, v if isinstance(v, int) else eng.to_reg(v)) for s, v in waits]
            eng.wait_ge(s_prepd, 1)
            for s, v in counts:
                eng.wait_ge(s, v)

        @block.sync
        def _(sp):
            for n, a in enumerate((a_src1, a_dst1)):
                sp.dma_start(hb[:, n, :], a.rearrange("(o h) f -> o (h f)", o=1).broadcast_to([P, HF])).then_inc(s_cin, 16)
            for n, a in enumerate((a_src2, a_dst2)):
                sp.dma_start(e2[:, 0, n, :], a.broadcast_to([P, D])).then_inc(s_cin, 16)
            sp.dma_start(b2b[:, :], b2.rearrange("(o d) -> o d", o=1).broadcast_to([P, D])).then_inc(s_cin, 16)
            sp.dma_start(b1T[:, :], b1.rearrange("(h f) -> f h", f=P), allow_slow_non_contiguous=True).then_inc(s_cin, 16)
            sp.dma_start(stage[:, 0, :].rearrange("p (k n) -> p k n", k=KD), W1.rearrange("(k p) n -> p k n", p=P)).then_inc(s_w12, 16)
            sp.dma_start(stage[:, 1, :].rearrange("p (k n) -> p k n", k=KF), W2.rearrange("(k p) n -> p k n", p=P)).then_inc(s_w12, 16)
            sp.wait_ge(s_cz, 1)
            sp.dma_start(t[:, 0:KD, 0:E], router_w.rearrange("(k p) e -> p k e", p=P)).then_inc(s_cin, 16)

            def load_graph(b, first=False):
                if not first:
                    sp.wait_ge(s_res, b)
                sp.dma_start(xb[:, :, :], x[bass.ds(b, 1)].rearrange("o (j p) d -> p (o j) d", p=P)).then_inc(s_x, 16)
                if not first:
                    sp.wait_ge(s_maskp, 2 * b)
                sp.dma_start(adjb[:, :, :], adj[bass.ds(b, 1)].rearrange("o (j p) d -> p (o j) d", p=P)).then_inc(s_adj, 16)

            def load_chunk(e, c, n, first=False):
                slot = (e * NW + c) % 2
                if not first:
                    sp.wait_ge(s_wl, n - 1)
                else:
                    sp.wait_ge(s_prepd, 1)
                dst = stage[:, slot, :].rearrange("p (k n) -> p k n", k=KD if c < 2 else FT)
                src = (w1, w3, w2)[c][e].rearrange("(k p) n -> p k n", p=P)
                sp.dma_start(dst, src).then_inc(s_wst[slot], 16)

            def load_expert(e, n0, first=False):
                for c in range(NW):
                    load_chunk(e, c, n0 + c, first and c < 2)

            load_graph(0, True)
            load_expert(0, 0, True)
            with sp.Fori(1, SB_B) as b:
                load_graph(b)

            def store(s, par):
                sp.wait_ge(s_y, NBLK * E * (s + 1))
                sp.dma_start(out[bass.ds(s * SB_B, SB_B)].rearrange("g (j p) d -> p (g j) d", p=P),
                             yacc[:, par * SB_B * NJ:(par + 1) * SB_B * NJ, :]).then_inc(s_out, 16)

            def iteration(s, q, last_sb, par):
                if not last_sb:
                    load_graph(s * SB_B + q + SB_B)
                load_expert(EI * q + 1, s * NW * E + NW * (EI * q + 1))
                if not (last_sb and q == SB_B - 1):
                    load_expert((EI * q + EI) % E, s * NW * E + NW * (EI * q + EI))

            with sp.Fori(0, NSB // 2 - 1) as sh:
                for par in range(2):
                    s = sh * 2 + par
                    for q in range(SB_B):
                        iteration(s, q, False, par)
                    store(s, par)
            for s, par in ((NSB - 2, 0), (NSB - 1, 1)):
                for q in range(SB_B):
                    iteration(s, q, s == NSB - 1, par)
                store(s, par)
            sp.wait_ge(s_out, 16 * NSB)

        AT = dict(inputs=0, norm1=0, T1=1, MT=1, RW=2, X1_0=2, CT=3, X1_1=4, SB0=4, SB1=5, bias2=3, max0=5, exp0=6,
                  prob0=7, max1=7, PT0=8, PT1=9, exp1=10, A1_0=10, prob1=11, PT2=12, elu0=11, PT3=13, A1_1=14, elu1=15,
                  h1=16, X2_0=17, X2_1=17, B2=19, max2=19, exp2=20, prob2=20, PT4=21, A2=22, x1=22, norm2=23, T2=24,
                  RT=25, LC=26, top=27, gap=27, comb=28, res=24)

        @block.gpsimd
        def _(pool):
            nc.gpsimd.memset(ident[:, :], 0.0)
            nc.gpsimd.memset(eye[:, :, :], 0.0)
            nc.gpsimd.memset(t[:, :, :], 0.0).then_inc(s_cz, 1)
            nc.gpsimd.memset(z[:, :, :], 0.0).then_inc(s_cz, 1)
            for e in range(E):
                nc.gpsimd.memset(expert_id[:, e:e + 1], float(e))
            pool.wait_ge(s_cz, 2)
            nc.gpsimd.affine_select(out=ident[:, :], in_=ident[:, :], compare_op=ALU.not_equal, fill=1.0, base=0,
                                    pattern=[[-1, P]], channel_multiplier=1)
            nc.gpsimd.affine_select(out=eye[:, :, :], in_=eye[:, :, :], compare_op=ALU.not_equal, fill=1.0, base=0,
                                    pattern=[[P, NJ], [-1, N]], channel_multiplier=1)
            spread = z[0:2 * H, 0:H, 0:P]
            nc.gpsimd.affine_select(out=spread, in_=spread, compare_op=ALU.not_equal, fill=1.0, base=0,
                                    pattern=[[-1, H], [0, P]], channel_multiplier=1).then_inc(s_cid, 1)
            pool.wait_ge(s_cid, 1)
            nc.gpsimd.tensor_copy(ident_r[:, :], ident[:, :])
            nc.gpsimd.tensor_copy(ident_b[:, :], ident[:, :])
            nc.gpsimd.tensor_copy(head_row[:, :, :], spread).then_inc(s_cr, 1)
            pool.sem_inc(s_hl, CREDIT)

            def split(el, c, i, ahead):
                k = NW * el + c
                dh, dl = (flat((we1, we3, we2)[c][el][s]) for s in range(2))
                wait_alone(pool, (s_wst[k % 2], 8 * NWI * (i + ahead) + 16 * (k // 2) + 16))
                nc.gpsimd.tensor_copy(dh, stage[:, k % 2, :]).then_inc(s_wh, 1)
                pool.wait_ge(s_wh, NWI * (i + ahead) + k + 1)
                nc.gpsimd.tensor_tensor(dl, stage[:, k % 2, :], dh, ALU.subtract).then_inc(s_wl, 1)

            def graph_inputs(b):
                wait_alone(pool, (s_adj, 16 * b + 16), (s_MT, b))
                nc.gpsimd.tensor_scalar(mask[:, :, :], adjb[:, :, :], 0.0, None, ALU.is_gt).then_inc(s_maskp, 1)
                pool.wait_ge(s_maskp, 2 * b + 1)
                nc.gpsimd.tensor_tensor(mask[:, :, :], mask[:, :, :], eye[:, :, :], ALU.add).then_inc(s_maskp, 1)
                wait_alone(pool, (s_maskp, 2 * b + 2))
                nc.gpsimd.tensor_scalar(mask[:, :, :], mask[:, :, :], 1.0, None, ALU.min).then_inc(s_mask, 1)

            def graph_bias(b):
                pool.wait_ge(s_ln1, b + 1)
                nc.gpsimd.tensor_tensor(xb[:, :, :], xb[:, :, :], b2b[:, :].unsqueeze(1).broadcast_to([P, NJ, D]),
                                        ALU.add).then_inc(s_xb2, 1)

            def graph_h1_low(b, g):
                pool.wait_ge(s_h1h, 2 * b + g + 1)
                hs = slice(2 * g, 2 * g + 2)
                nc.gpsimd.tensor_tensor(h1s[1][:, hs, :], z[:, hs, :], h1s[0][:, hs, :], ALU.subtract).then_inc(s_h1, 1)

            def graph_residual(b, p, par, base):
                stored = [] if base is None else [(s_out, base * (16 // SB_B))]
                wait_alone(pool, (s_ln2, b + 1), *stored)
                nc.gpsimd.tensor_copy(yacc[:, bass.ds(p * NJ + par * SB_B * NJ, NJ), :], xb[:, :, :]).then_inc(s_res, 1)

            def graph_phase(b, p, par, base, ph):
                if ph == AT["inputs"]:
                    graph_inputs(b)
                if ph == AT["bias2"]:
                    graph_bias(b)
                if ph == AT["h1"]:
                    graph_h1_low(b, 0)
                    graph_h1_low(b, 1)
                if ph == AT["res"]:
                    graph_residual(b, p, par, base)

            def hidden_low(i, u):
                pool.wait_ge(s_hh, UNITS * i + u + 1)
                nc.gpsimd.tensor_tensor(hhs[1][:, u % 2, :], hb[:, u % 2, :], hhs[0][:, u % 2, :],
                                        ALU.subtract).then_inc(s_hl, 1)

            def graph_only(b, p, par):
                for ph in range(2 * UNITS):
                    graph_phase(b, p, par, None, ph)

            def ffn(base, p, par, graph=True, last=False):
                i = base + p
                half = UNITS // 2
                for u in range(UNITS):
                    if graph:
                        graph_phase(i + SB_B, p, 1 - par, base, 2 * u)
                    if u == 1:
                        pool.wait_ge(s_dn, UNITS * i + CREDIT)
                    if 1 <= u <= NW:
                        split(1, u - 1, i, 0)
                    hidden_low(i, u)
                    if u == half + 2:
                        pool.wait_ge(s_dn, UNITS * i + half + CREDIT)
                    if half + 2 <= u < half + 2 + NW and not last:
                        split(0, u - half - 2, i, 1)
                    if graph:
                        graph_phase(i + SB_B, p, 1 - par, base, 2 * u + 1)

            pool.wait_ge(s_prepd, 1)
            for c in range(NW):
                split(0, c, 0, 0)
            run_iterations(pool, graph_only, ffn)

        @block.scalar
        def _(act):
            def nT_high(b):
                act.wait_ge(s_T1, b + 1)
                act.wait_ge(s_A2, b)
                nc.scalar.activation(flat(nTs[0]), pA[:, :], ACT.Copy).then_inc(s_nTh, 1)

            def mask_bias(b):
                act.wait_ge(s_MT, b + 1)
                act.wait_ge(s_max, 3 * b)
                nc.scalar.activation(flat(mbias), maskT, ACT.Copy, bias=-MASKED, scale=MASKED).then_inc(s_mb, 1)

            def rows_copy(b):
                act.wait_ge(s_RW, b + 1)
                act.wait_ge(s_SB, 2 * b)
                nc.scalar.activation(rows_f[:, :], pA[0:2 * H, 0:N], ACT.Copy)
                nc.scalar.activation(rows_s[0][:, :], pA[0:2 * H, 0:N], ACT.Copy).then_inc(s_rwc, 1)

            def features1_high(b, j):
                act.wait_ge(s_X1, 2 * b + j + 1)
                act.wait_ge(s_A1, H * b)
                nc.scalar.activation(xls[0][:, j, :], pB[:, :], ACT.Copy).then_inc(s_xlh, 1)

            def exps(b, g):
                act.wait_ge(s_max, 3 * b + g + 1)
                act.wait_ge(s_PT, (H + 1) * b + 2 * g)
                for h in range(2 if g < 2 else 1):
                    for j in range(NJ):
                        nc.scalar.activation(e1[:, h, j, :], sc[:, h, j, :], ACT.Exp, bias=bi1[:, j, h:h + 1])
                        last = nc.scalar.activation(e2[:, h, j, :], sc[:, h, j, :], ACT.Exp, bias=bi2[:, j, h:h + 1],
                                                    scale=NEG_SLOPE)
                last.then_inc(s_exp, 1)

            def probs_high(b, h):
                act.wait_ge(s_PT, (H + 1) * b + h + 1)
                if h == 0:
                    act.wait_ge(s_A2, b)
                else:
                    act.wait_ge(s_A1, H * b + max(h - 1, 0))
                nc.scalar.activation(PTs[0][:, h % 2, :, :].rearrange("p j n -> p (j n)"), bank_PT[h][:, :],
                                     ACT.Copy).then_inc(s_PTh, 1)

            def attended_bias(b, g):
                act.wait_ge(s_A1, H * b + 2 * g + 2)
                act.wait_ge(s_h1, 2 * b)
                for h in range(2):
                    last = nc.scalar.activation(z[:, 2 * g + h, :], bank_A1[g][:, h * N:(h + 1) * N], ACT.Identity,
                                                bias=b1T[:, 2 * g + h:2 * g + h + 1])
                last.then_inc(s_z, 1)

            def elu_exp(b, g):
                act.wait_ge(s_zn, 2 * b + g + 1)
                nc.scalar.activation(t[:, 2 * g:2 * g + 2, :], t[:, 2 * g:2 * g + 2, :], ACT.Exp).then_inc(s_ze, 1)

            def h1_high(b, g):
                act.wait_ge(s_zf, 2 * b + g + 1)
                act.wait_ge(s_X2, 2 * b)
                nc.scalar.activation(h1s[0][:, 2 * g:2 * g + 2, :], z[:, 2 * g:2 * g + 2, :], ACT.Copy).then_inc(s_h1h, 1)

            def features2_high(b, j):
                act.wait_ge(s_X2, 2 * b + j + 1)
                nc.scalar.activation(nTs[0][:, j, :], bank_X2[j][:, 0:D], ACT.Copy).then_inc(s_x2h, 1)

            def ffn_x_high(b, p, par):
                act.wait_ge(s_T2, b + 1)
                nc.scalar.activation(xTs[0][:, :, bass.ds(p * N + par * SB_T, N)], fold(pB), ACT.Copy).then_inc(s_fTh, 1)

            def router_rows(b):
                act.wait_ge(s_RT, b + 1)
                nc.scalar.activation(lrows[:, :], pA[0:E, 0:N], ACT.Copy).then_inc(s_lr, 1)

            def gap_exp(b):
                act.wait_ge(s_gap, b + 1)
                nc.scalar.activation(eg[:, :], gap[:, :], ACT.Exp).then_inc(s_eg, 1)

            def graph_phase(b, p, par, ph):
                if ph == AT["T1"]:
                    nT_high(b)
                if ph == AT["MT"]:
                    mask_bias(b)
                if ph == AT["RW"]:
                    rows_copy(b)
                if ph == AT["X1_0"]:
                    features1_high(b, 0)
                if ph == AT["X1_1"]:
                    features1_high(b, 1)
                if ph == AT["exp0"]:
                    exps(b, 0)
                if ph == AT["PT0"]:
                    probs_high(b, 0)
                if ph == AT["PT1"]:
                    probs_high(b, 1)
                if ph == AT["exp1"]:
                    exps(b, 1)
                if ph == AT["elu0"]:
                    attended_bias(b, 0)
                    elu_exp(b, 0)
                if ph == AT["PT2"]:
                    probs_high(b, 2)
                if ph == AT["PT3"]:
                    probs_high(b, 3)
                if ph == AT["elu1"]:
                    attended_bias(b, 1)
                    elu_exp(b, 1)
                if ph == AT["h1"]:
                    h1_high(b, 0)
                    h1_high(b, 1)
                if ph == AT["X2_0"]:
                    features2_high(b, 0)
                if ph == AT["X2_1"]:
                    features2_high(b, 1)
                if ph == AT["exp2"]:
                    exps(b, 2)
                if ph == AT["PT4"]:
                    probs_high(b, H)
                if ph == AT["T2"]:
                    ffn_x_high(b, p, par)
                if ph == AT["RT"]:
                    router_rows(b)
                if ph == AT["gap"]:
                    gap_exp(b)

            def gate_tanh(i, u):
                act.wait_ge(s_g, UNITS * i + u + 1)
                act.wait_ge(s_hl, UNITS * i + u + 1)
                nc.scalar.activation(hb[:, u % 2, :], pG[u % 2][:, :], ACT.Tanh, scale=0.5).then_inc(s_th, 1)

            def hidden_high(i, u):
                act.wait_ge(s_h, UNITS * i + u + 1 + CREDIT)
                act.wait_ge(s_dn, UNITS * i + u + 1)
                nc.scalar.activation(hhs[0][:, u % 2, :], hb[:, u % 2, :], ACT.Copy).then_inc(s_hh, 1)

            def graph_only(b, p, par):
                for ph in range(2 * UNITS):
                    graph_phase(b, p, par, ph)

            def ffn(base, p, par, graph=True, last=False):
                i = base + p
                for u in range(UNITS):
                    gate_tanh(i, u)
                    if graph:
                        graph_phase(i + SB_B, p, 1 - par, 2 * u)
                    hidden_high(i, u)
                    if graph:
                        graph_phase(i + SB_B, p, 1 - par, 2 * u + 1)

            act.wait_ge(s_prepd, 1)
            run_iterations(act, graph_only, ffn)

        @block.vector
        def _(dve):
            prepared = [0]

            def prep(ins):
                prepared[0] += 1
                ins.then_inc(s_prep, 1)
                dve.wait_ge(s_prep, prepared[0])

            dve.wait_ge(s_w12, 32)
            dve.wait_ge(s_cz, 2)
            dve.wait_ge(s_cin, 16 * 7)
            nc.vector.tensor_copy(flat(W1s[0]), stage[:, 0, :])
            prep(nc.vector.tensor_copy(W2s[0][:, :, 0:D], fold(stage[:, 1, :], KF)))
            nc.vector.tensor_tensor(flat(W1s[1]), stage[:, 0, :], flat(W1s[0]), ALU.subtract)
            nc.vector.tensor_tensor(W2s[1][:, :, 0:D], fold(stage[:, 1, :], KF), W2s[0][:, :, 0:D], ALU.subtract)
            tmp = sc[:, :, :, :].rearrange("p a j n -> p (a j n)")
            for k in range(KD):
                for n in range(2):
                    prep(nc.vector.tensor_tensor(tmp[:, 0:HF], stage[:, 0, k * HF:(k + 1) * HF], hb[:, n, :], ALU.mult))
                    prep(nc.vector.tensor_reduce(t[:, KD + k, n * H:(n + 1) * H],
                                                 tmp[:, 0:HF].rearrange("p (h f) -> p h f", h=H), AX_X, ALU.add))
            for n in range(2):
                w = tmp[:, 0:KF * D].rearrange("p (k n) -> p k n", k=KF)
                prep(nc.vector.tensor_tensor(w, fold(stage[:, 1, :], KF),
                                             e2[:, 0, n, :].unsqueeze(1).broadcast_to([P, KF, D]), ALU.mult))
                prep(nc.vector.tensor_reduce(v2f[:, :, n], w, AX_X, ALU.add))
            nc.vector.tensor_copy(rws[0][:, :, :], t[:, 0:KD, 0:P])
            nc.vector.tensor_copy(v1s[0][:, :, :], t[:, KD:2 * KD, 0:P])
            prep(nc.vector.tensor_copy(W2s[0][:, :, D:W2N], v2f[:, :, :]))
            nc.vector.tensor_tensor(rws[1][:, :, :], t[:, 0:KD, 0:P], rws[0][:, :, :], ALU.subtract)
            nc.vector.tensor_tensor(v1s[1][:, :, :], t[:, KD:2 * KD, 0:P], v1s[0][:, :, :], ALU.subtract)
            nc.vector.tensor_tensor(W2s[1][:, :, D:W2N], v2f[:, :, :], W2s[0][:, :, D:W2N],
                                    ALU.subtract).then_inc(s_prepd, 1)
            dve.sem_inc(s_a, CREDIT)
            dve.sem_inc(s_h, CREDIT)

            links = [0]

            def link(ins, b, alone=False):
                links[0] += 1
                ins.then_inc(s_dg, 1)
                if alone:
                    wait_alone(dve, (s_dg, DVE_LINKS * b + links[0]))
                else:
                    dve.wait_ge(s_dg, DVE_LINKS * b + links[0])

            def layer_norm(b, src, done):
                for j in range(NJ):
                    last = nc.vector.bn_stats(st[:, j, :], src[:, j, :])
                link(last, b, alone=True)
                for j in range(NJ):
                    last = nc.vector.bn_aggr(mv[:, j, :], st[:, j, :])
                link(last, b)
                v, y, s, r = (nw[:, k, :] for k in range(4))
                link(nc.vector.tensor_scalar(v, mv[:, :, 1], LN_EPS, None, ALU.add), b)
                link(nc.vector.tensor_scalar(s.bitcast(I32), v.bitcast(I32), 1, None, ALU.arith_shift_right), b)
                link(nc.vector.tensor_scalar(y.bitcast(I32), s.bitcast(I32), -1.0, RSQRT_SEED, ALU.mult, ALU.add), b)
                for _ in range(NEWTON_STEPS):
                    link(nc.vector.tensor_tensor(s, y, y, ALU.mult), b)
                    link(nc.vector.tensor_tensor(r, s, v, ALU.mult), b)
                    link(nc.vector.tensor_scalar(r, r, -0.5, 1.5, ALU.mult, ALU.add), b)
                    link(nc.vector.tensor_tensor(y, y, r, ALU.mult), b)
                for j in range(NJ):
                    last = nc.vector.tensor_scalar(xn[:, j, :], src[:, j, :], mv[:, j, 0:1], y[:, j:j + 1],
                                                   ALU.subtract, ALU.mult)
                last.then_inc(done, 1)

            def norm1(b):
                dve.wait_ge(s_x, 16 * b + 16)
                layer_norm(b, xb, s_ln1)

            def nT_low(b):
                dve.wait_ge(s_nTh, b + 1)
                nc.vector.tensor_tensor(flat(nTs[1]), pA[:, :], flat(nTs[0]), ALU.subtract).then_inc(s_nT, 1)

            def rows_low(b):
                dve.wait_ge(s_rwc, b + 1)
                nc.vector.tensor_tensor(rows_s[1][:, :], pA[0:2 * H, 0:N], rows_s[0][:, :], ALU.subtract).then_inc(s_rwl, 1)

            def cols_copy(b):
                dve.wait_ge(s_CT, b + 1)
                nc.vector.tensor_copy(flat(cols), pA[:, 0:NJ * 2 * H]).then_inc(s_cols, 1)

            def features1_low(b, j):
                dve.wait_ge(s_xlh, 2 * b + j + 1)
                nc.vector.tensor_tensor(xls[1][:, j, :], pB[:, :], xls[0][:, j, :], ALU.subtract).then_inc(s_xll, 1)

            def softmax_max(b, g):
                exps_done = (s_exp, 3 * b + g)
                if g < 2:
                    wait_alone(dve, exps_done, (s_SB, 2 * b + g + 1), (s_mb, b + 1), (s_cols, b + 1))
                    spread, target, nh = (pA, pB)[g], cols[:, :, H + 2 * g:H + 2 * g + 2], 2
                else:
                    wait_alone(dve, exps_done, (s_B2, b + 1))
                    spread, target, nh = pA, a2c[:, :, 1:2], 1
                for h in range(nh):
                    for j in range(NJ):
                        last = nc.vector.tensor_tensor_reduce(sc[:, h, j, :], spread[:, h * N:(h + 1) * N], mbias[:, j, :],
                                                              1.0, LOWEST, ALU.add, ALU.max, mx[:, j, h:h + 1])
                link(last, b)
                m, mt = mm_[:, :, 0:nh], mx[:, :, 0:nh]
                link(nc.vector.tensor_tensor(mt, mt, target, ALU.add), b)
                link(nc.vector.scalar_tensor_tensor(m, mt, NEG_SLOPE, mt, ALU.mult, ALU.max), b)
                nc.vector.tensor_tensor(bi1[:, :, 0:nh], target, m, ALU.subtract)
                nc.vector.scalar_tensor_tensor(bi2[:, :, 0:nh], target, NEG_SLOPE, m, ALU.mult,
                                               ALU.subtract).then_inc(s_max, 1)

            def softmax_probs(b, g):
                dve.wait_ge(s_exp, 3 * b + g + 1)
                nh = 2 if g < 2 else 1
                for h in range(nh):
                    for j in range(NJ):
                        last = nc.vector.scalar_tensor_tensor(e1[:, h, j, :], e1[:, h, j, :], 1.0, e2[:, h, j, :], ALU.mult,
                                                              ALU.max, accum_out=sm[:, j, h:h + 1])
                if g == 2:
                    last.then_inc(s_pn, 1)
                    dve.wait_ge(s_pn, 3 * b + 3)
                    nc.vector.reciprocal(rs[:, :, 0:1], sm[:, :, 0:1])
                    return
                link(last, b)
                link(nc.vector.reciprocal(rs[:, :, :], sm[:, :, :]), b)
                for h in range(nh):
                    for j in range(NJ):
                        last = nc.vector.tensor_scalar(e1[:, h, j, :], e1[:, h, j, :], rs[:, j, h:h + 1], None, ALU.mult)
                last.then_inc(s_pn, 1)

            def probs_low(b, h):
                dve.wait_ge(s_PTh, (H + 1) * b + h + 1)
                dst = (pt[:, h % 2, :, :].rearrange("p j n -> p (j n)") for pt in PTs)
                hi, lo = dst
                nc.vector.tensor_tensor(lo, bank_PT[h][:, :], hi, ALU.subtract).then_inc(s_PTl, 1)

            def elu_negative(b, g):
                dve.wait_ge(s_z, 2 * b + g + 1)
                zs, ts = z[:, 2 * g:2 * g + 2, :], t[:, 2 * g:2 * g + 2, :]
                nc.vector.tensor_scalar(ts, zs, 0.0, None, ALU.min).then_inc(s_zn, 1)
                dve.wait_ge(s_zn, 2 * b + g + 1)
                link(nc.vector.tensor_scalar(zs, zs, 0.0, None, ALU.max), b)

            def elu_sum(b, g):
                dve.wait_ge(s_ze, 2 * b + g + 1)
                zs, ts = z[:, 2 * g:2 * g + 2, :], t[:, 2 * g:2 * g + 2, :]
                nc.vector.scalar_tensor_tensor(zs.rearrange("p a b -> p (a b)"), ts.rearrange("p a b -> p (a b)"), -1.0,
                                               zs.rearrange("p a b -> p (a b)"), ALU.add, ALU.add).then_inc(s_zf, 1)

            def features2_low(b, j):
                dve.wait_ge(s_x2h, 2 * b + j + 1)
                nc.vector.tensor_copy(a2c[:, j, :], bank_X2[j][:, D:W2N])
                nc.vector.tensor_tensor(nTs[1][:, j, :], bank_X2[j][:, 0:D], nTs[0][:, j, :], ALU.subtract).then_inc(s_x2l, 1)

            def source2(b):
                dve.wait_ge(s_x2l, 2 * b + 2)
                src = a2c[:, :, 0:1].broadcast_to([P, NJ, P])
                link(nc.vector.tensor_copy(a2s[0][:, :, :], src), b)
                nc.vector.tensor_tensor(a2s[1][:, :, :], src, a2s[0][:, :, :], ALU.subtract).then_inc(s_a2, 1)

            def residual1(b):
                dve.wait_ge(s_A2, b + 1)
                dve.wait_ge(s_xb2, b + 1)
                for j in range(NJ):
                    last = nc.vector.scalar_tensor_tensor(xb[:, j, :], pA[:, j * D:(j + 1) * D], rs[:, j, 0:1],
                                                          xb[:, j, :], ALU.mult, ALU.add)
                last.then_inc(s_x1, 1)
                dve.wait_ge(s_x1, b + 1)

            def ffn_x_low(b, p, par):
                dve.wait_ge(s_fTh, b + 1)
                at = bass.ds(p * N + par * SB_T, N)
                nc.vector.tensor_tensor(xTs[1][:, :, at], fold(pB), xTs[0][:, :, at], ALU.subtract).then_inc(s_fT, 1)

            def router_top(b):
                dve.wait_ge(s_LC, b + 1)
                nc.vector.tensor_copy(flat(lg), pB[:, 0:NJ * E]).then_inc(s_lg, 1)
                wait_alone(dve, (s_lg, b + 1))
                for j in range(NJ):
                    last = nc.vector.max(top[:, j, :], lg[:, j, :])
                link(last, b)
                nc.vector.tensor_tensor(gap[:, :], top[:, :, 1], top[:, :, 0], ALU.subtract).then_inc(s_gap, 1)
                for j in range(NJ):
                    last = nc.vector.max_index(topi[:, j, :], top[:, j, :], lg[:, j, :])
                link(last, b)
                link(nc.vector.tensor_copy(flat(topf), flat(topi)), b)

            def router_weights(b, p, par):
                dve.wait_ge(s_eg, b + 1)
                s, w0, w1_ = (wts[:, k, :] for k in range(3))
                link(nc.vector.tensor_scalar(s, eg[:, :], 2.0, 2.0, ALU.mult, ALU.add), b)
                link(nc.vector.reciprocal(w0, s), b)
                link(nc.vector.tensor_tensor(w1_, eg[:, :], w0, ALU.mult), b)
                for j in range(NJ):
                    for k, w in enumerate((w0, w1_)):
                        last = nc.vector.tensor_scalar(oh[:, k, j, :], expert_id[:, :], topf[:, j, k:k + 1], w[:, j:j + 1],
                                                       ALU.is_equal, ALU.mult)
                link(last, b)
                nc.vector.tensor_tensor(comb[:, bass.ds(p * NJ + par * SB_B * NJ, NJ), :], oh[:, 0, :, :], oh[:, 1, :, :],
                                        ALU.add).then_inc(s_comb, 1)

            def graph_phase(b, p, par, ph):
                if ph == AT["norm1"]:
                    norm1(b)
                if ph == AT["T1"]:
                    nT_low(b)
                if ph == AT["RW"]:
                    rows_low(b)
                if ph == AT["X1_0"]:
                    features1_low(b, 0)
                if ph == AT["CT"]:
                    cols_copy(b)
                if ph == AT["X1_1"]:
                    features1_low(b, 1)
                if ph == AT["max0"]:
                    softmax_max(b, 0)
                if ph == AT["prob0"]:
                    softmax_probs(b, 0)
                if ph == AT["max1"]:
                    softmax_max(b, 1)
                if ph == AT["PT0"]:
                    probs_low(b, 0)
                if ph == AT["PT1"]:
                    probs_low(b, 1)
                if ph == AT["prob1"]:
                    softmax_probs(b, 1)
                if ph == AT["elu0"]:
                    elu_negative(b, 0)
                if ph == AT["PT2"]:
                    probs_low(b, 2)
                    elu_sum(b, 0)
                if ph == AT["PT3"]:
                    probs_low(b, 3)
                if ph == AT["elu1"]:
                    elu_negative(b, 1)
                    elu_sum(b, 1)
                if ph == AT["X2_0"]:
                    features2_low(b, 0)
                if ph == AT["X2_1"]:
                    features2_low(b, 1)
                    source2(b)
                if ph == AT["max2"]:
                    softmax_max(b, 2)
                if ph == AT["prob2"]:
                    softmax_probs(b, 2)
                if ph == AT["PT4"]:
                    probs_low(b, H)
                if ph == AT["x1"]:
                    residual1(b)
                if ph == AT["norm2"]:
                    layer_norm(b, xb, s_ln2)
                if ph == AT["T2"]:
                    ffn_x_low(b, p, par)
                if ph == AT["top"]:
                    router_top(b)
                if ph == AT["comb"]:
                    router_weights(b, p, par)

            def pair_weights(i, base, p, par):
                dve.wait_ge(s_comb, base + SB_B)
                dve.wait_ge(s_y, GROUPS * i)
                nc.vector.tensor_copy(cw[:, :, :], comb[:, par * SB_B * NJ:(par + 1) * SB_B * NJ,
                                                        bass.ds(p * EI, EI)]).then_inc(s_cw, 1)
                dve.wait_ge(s_cw, i + 1)
                dve.wait_ge(s_res, base + SB_B)

            def gate_product(i, u):
                dve.wait_ge(s_th, UNITS * i + u + 1)
                hu = hb[:, u % 2, :]
                nc.vector.scalar_tensor_tensor(hu, hu, 1.0, pG[u % 2][:, :], ALU.add, ALU.mult).then_inc(s_a, 1)

            def hidden(i, u):
                dve.wait_ge(s_u, UNITS * i + u + 1)
                dve.wait_ge(s_a, UNITS * i + u + 1 + CREDIT)
                hu = hb[:, u % 2, :]
                nc.vector.tensor_tensor(hu, hu, pU[u % 2][:, :], ALU.mult).then_inc(s_h, 1)

            def add_y(i, g, par):
                el, blk = divmod(g, NBLK)
                dve.wait_ge(s_dn, UNITS * i + (g + 1) * FT + CREDIT)
                dve.wait_ge(s_y, GROUPS * i + g)
                for tt in range(TT):
                    tile = blk * TT + tt
                    acc = yacc[:, par * SB_B * NJ + tile, :]
                    last = nc.vector.scalar_tensor_tensor(acc, pY[tt // 2][:, tt % 2, :], cw[:, tile, el:el + 1], acc,
                                                          ALU.mult, ALU.add)
                last.then_inc(s_y, 1)

            def graph_only(b, p, par):
                links[0] = 0
                for ph in range(2 * UNITS):
                    graph_phase(b, p, par, ph)
                assert links[0] == DVE_LINKS, links[0]

            def ffn(base, p, par, graph=True, last=False):
                i = base + p
                links[0] = 0
                pair_weights(i, base, p, par)
                for u in range(UNITS):
                    gate_product(i, u)
                    if graph:
                        graph_phase(i + SB_B, p, 1 - par, 2 * u)
                    hidden(i, u)
                    if graph:
                        graph_phase(i + SB_B, p, 1 - par, 2 * u + 1)
                    if u % FT == LAG - 1 and u >= FT:
                        add_y(i, u // FT - 1, par)
                add_y(i, GROUPS - 1, par)

            run_iterations(dve, graph_only, ffn)

        @block.tensor
        def _(pe):
            def pairs(a, b):
                return ((a[0], b[0]), (a[1], b[0]), (a[0], b[1]))

            def product(dst, terms):
                for n, (lhsT, rhs) in enumerate(terms):
                    last = nc.tensor.matmul(dst, lhsT, rhs, start=(n == 0), stop=(n == len(terms) - 1))
                return last

            def transpose_norm(b, bank, done):
                for k in range(KD):
                    for j in range(NJ):
                        last = nc.tensor.transpose(bank[:, k * N + j * P:k * N + (j + 1) * P], xn[:, j, k * P:(k + 1) * P],
                                                   ident[:, :])
                last.then_inc(done, 1)

            def T1(b):
                pe.wait_ge(s_ln1, b + 1)
                pe.wait_ge(s_lr, b)
                transpose_norm(b, pA, s_T1)

            def MT(b):
                pe.wait_ge(s_mask, b + 1)
                pe.wait_ge(s_lg, b)
                for jt in range(NJ):
                    for js in range(NJ):
                        last = nc.tensor.transpose(maskT[:, jt * N + js * P:jt * N + (js + 1) * P],
                                                   mask[:, js, jt * P:(jt + 1) * P], ident_b[:, :])
                last.then_inc(s_MT, 1)

            def RW(b):
                pe.wait_ge(s_nT, b + 1)
                product(pA[:, 0:N], [(v[:, k, :], n[:, k, :]) for k in range(KD) for v, n in pairs(v1s, nTs)]).then_inc(s_RW, 1)

            def X1(b, j):
                if j == 0:
                    pe.wait_ge(s_mb, b + 1)
                else:
                    pe.wait_ge(s_xll, 2 * b + 1)
                product(pB[:, :], [(n[:, k, j * P:(j + 1) * P], w[:, k, :]) for k in range(KD)
                                   for n, w in pairs(nTs, W1s)]).then_inc(s_X1, 1)

            def CT(b):
                wait_alone(pe, (s_rwl, b + 1))
                for j in range(NJ):
                    last = nc.tensor.transpose(pA[:, j * 2 * H:(j + 1) * 2 * H], rows_f[:, j * P:(j + 1) * P],
                                               ident[0:2 * H, 0:2 * H])
                last.then_inc(s_CT, 1)

            def SB(b, g):
                if g == 0:
                    pe.wait_ge(s_cols, b + 1)
                else:
                    pe.wait_ge(s_xll, 2 * b + 2)
                for h in range(2):
                    last = product((pA, pB)[g][:, h * N:(h + 1) * N],
                                   [(head_row[:, 2 * g + h, :], r[:, :]) for r in rows_s])
                last.then_inc(s_SB, 1)

            def PT(b, h):
                if h in (0, 1):
                    pe.wait_ge(s_pn, 3 * b + 1)
                    pe.wait_ge(s_max, 3 * b + h + 1)
                elif h in (2, 3):
                    pe.wait_ge(s_pn, 3 * b + 2)
                    if h == 2:
                        pe.wait_ge(s_PTl, 5 * b + 2)
                    else:
                        pe.wait_ge(s_z, 2 * b + 1)
                else:
                    pe.wait_ge(s_pn, 3 * b + 3)
                    pe.wait_ge(s_x2l, 2 * b + 2)
                for js in range(NJ):
                    for jt in range(NJ):
                        last = nc.tensor.transpose(bank_PT[h][:, js * N + jt * P:js * N + (jt + 1) * P],
                                                   e1[:, h % 2, jt, js * P:(js + 1) * P], ident[:, :])
                last.then_inc(s_PT, 1)

            def A1(b, h):
                pe.wait_ge(s_PTl, 5 * b + h + 1)
                if h == 2:
                    pe.wait_ge(s_PTl, 5 * b + 3)
                product(bank_A1[h // 2][:, (h % 2) * N:(h % 2 + 1) * N],
                        [(xl[:, j, h * P:(h + 1) * P], pt[:, h % 2, j, :]) for j in range(NJ)
                         for xl, pt in pairs(xls, PTs)]).then_inc(s_A1, 1)

            def X2(b, j):
                pe.wait_ge(s_h1, 2 * b + 2)
                product(bank_X2[j][:, 0:W2N], [(h[:, k, j * P:(j + 1) * P], w[:, k, :]) for k in range(KF)
                                               for h, w in pairs(h1s, W2s)]).then_inc(s_X2, 1)

            def B2(b):
                pe.wait_ge(s_a2, b + 1)
                for j in range(NJ):
                    last = product(pA[:, j * P:(j + 1) * P], [(a[:, j, :], ident_r[:, :]) for a in a2s])
                last.then_inc(s_B2, 1)

            def A2(b):
                pe.wait_ge(s_PTl, 5 * b + 5)
                pe.wait_ge(s_max, 3 * b + 3)
                for jt in range(NJ):
                    last = product(pA[:, jt * D:(jt + 1) * D], [(pt[:, 0, js, jt * P:(jt + 1) * P], xl[:, js, :])
                                                                for js in range(NJ) for pt, xl in pairs(PTs, nTs)])
                last.then_inc(s_A2, 1)

            def T2(b):
                pe.wait_ge(s_ln2, b + 1)
                transpose_norm(b, pB, s_T2)

            def RT(b, p, par):
                pe.wait_ge(s_fT, b + 1)
                at = bass.ds(p * N + par * SB_T, N)
                product(pA[:, 0:N], [(r[:, k, :], xt[:, k, at]) for k in range(KD) for r, xt in pairs(rws, xTs)]).then_inc(s_RT, 1)

            def LC(b):
                wait_alone(pe, (s_lr, b + 1))
                for j in range(NJ):
                    last = nc.tensor.transpose(pB[:, j * E:(j + 1) * E], lrows[:, j * P:(j + 1) * P], ident[0:E, 0:E])
                last.then_inc(s_LC, 1)

            def graph_phase(b, p, par, ph):
                if ph == AT["T1"]:
                    T1(b)
                if ph == AT["MT"]:
                    MT(b)
                if ph == AT["RW"]:
                    RW(b)
                if ph == AT["X1_0"]:
                    X1(b, 0)
                if ph == AT["CT"]:
                    CT(b)
                if ph == AT["X1_1"]:
                    X1(b, 1)
                if ph == AT["SB0"]:
                    SB(b, 0)
                if ph == AT["SB1"]:
                    SB(b, 1)
                if ph == AT["PT0"]:
                    PT(b, 0)
                if ph == AT["PT1"]:
                    PT(b, 1)
                if ph == AT["A1_0"]:
                    A1(b, 0)
                    A1(b, 1)
                if ph == AT["PT2"]:
                    PT(b, 2)
                if ph == AT["PT3"]:
                    PT(b, 3)
                if ph == AT["A1_1"]:
                    A1(b, 2)
                    A1(b, 3)
                if ph == AT["X2_0"]:
                    X2(b, 0)
                if ph == AT["X2_1"]:
                    X2(b, 1)
                if ph == AT["B2"]:
                    B2(b)
                if ph == AT["PT4"]:
                    PT(b, H)
                if ph == AT["A2"]:
                    A2(b)
                if ph == AT["T2"]:
                    T2(b)
                if ph == AT["RT"]:
                    RT(b, p, par)
                if ph == AT["LC"]:
                    LC(b)

            def gate_up(i, u, par):
                el, blk, ft = u // (NBLK * FT), u // FT % NBLK, u % FT
                at = slice(par * SB_T + blk * BLK, par * SB_T + (blk + 1) * BLK)
                fs = slice(ft * P, (ft + 1) * P)
                for c, (we, bank, free, done) in enumerate(((we1, pG, s_a, s_g), (we3, pU, s_h, s_u))):
                    if u % (NBLK * FT) == 0:
                        pe.wait_ge(s_wl, NWI * i + NW * el + c + 1)
                    pe.wait_ge(free, UNITS * i + u + 1)
                    product(bank[u % 2][:, :], [(w[:, k, fs], xt[:, k, at]) for k in range(KD)
                                                for w, xt in pairs(we[el], xTs)]).then_inc(done, 1)

            def down(i, u):
                el, ft = u // (NBLK * FT), u % FT
                if u % (NBLK * FT) == 0:
                    pe.wait_ge(s_wl, NWI * i + NW * el + NW)
                if ft == 0:
                    pe.wait_ge(s_y, GROUPS * i + u // FT)
                pe.wait_ge(s_hl, UNITS * i + u + 1 + CREDIT)
                for tt in range(TT):
                    ts = slice(tt * P, (tt + 1) * P)
                    for n, (h, w) in enumerate(pairs(hhs, we2[el])):
                        last = nc.tensor.matmul(pY[tt // 2][:, tt % 2, :], h[:, u % 2, ts], w[:, ft, :],
                                                start=(ft == 0 and n == 0 and tt % 2 == 0),
                                                stop=(ft == FT - 1 and n == 2), skip_group_check=True)
                last.then_inc(s_dn, 1)

            def graph_only(b, p, par):
                for ph in range(2 * UNITS):
                    graph_phase(b, p, par, ph)

            def ffn(base, p, par, graph=True, last=False):
                i = base + p
                pe.wait_ge(s_fT, base + SB_B)
                for u in range(UNITS):
                    gate_up(i, u, par)
                    if graph:
                        graph_phase(i + SB_B, p, 1 - par, 2 * u)
                    if u >= LAG:
                        down(i, u - LAG)
                    if graph:
                        graph_phase(i + SB_B, p, 1 - par, 2 * u + 1)
                for u in range(UNITS - LAG, UNITS):
                    down(i, u)

            pe.sem_inc(s_dn, CREDIT)
            pe.wait_ge(s_prepd, 1)
            pe.wait_ge(s_cr, 1)
            run_iterations(pe, graph_only, ffn)


_INS = ['x', 'adj', 'L0_gnn_W1', 'L0_gnn_att_src1', 'L0_gnn_att_dst1', 'L0_gnn_b1', 'L0_gnn_W2', 'L0_gnn_att_src2',
        'L0_gnn_att_dst2', 'L0_gnn_b2', 'L0_ffn_router_w', 'L0_ffn_w1', 'L0_ffn_w2', 'L0_ffn_w3']
_OUTS = [((32, 256, 256), 'float32')]


def kernel(**inputs):
    import numpy as _np
    import concourse.bacc as _bacc
    from concourse import mybir as _mybir
    from concourse.bass_utils import run_bass_kernel_spmd as _run

    nc = _bacc.Bacc("TRN2", target_bir_lowering=False, num_devices=1)
    arrays, args = {}, []
    for name in _INS:
        a = _np.ascontiguousarray(inputs[name])
        arrays[f"in_{name}_dram"] = a
        args.append(nc.dram_tensor(f"in_{name}_dram", a.shape, _mybir.dt.from_np(a.dtype), kind="ExternalInput").ap())
    for i, (shape, dtype) in enumerate(_OUTS):
        dt = _mybir.dt.from_np(_np.dtype(dtype))
        args.append(nc.dram_tensor(f"out_{i}_dram", shape, dt, kind="ExternalOutput").ap())
    gat_moe_kernel(nc, *args)
    r = _run(nc, [arrays], core_ids=[0])
    got = tuple(r.results[0][f"out_{i}_dram"] for i in range(len(_OUTS)))
    return got[0]
```

```python
from contextlib import ExitStack

import concourse.bass as bass
from concourse import mybir

ALU = mybir.AluOpType
ACT = mybir.ActivationFunctionType
F32 = mybir.dt.float32
F32R = mybir.dt.float32r
BF16 = mybir.dt.bfloat16
I32 = mybir.dt.int32
U32 = mybir.dt.uint32
AX_X = mybir.AxisListType.X

P = 128
NEG_SLOPE = 0.2
LN_EPS = 1e-5
MASKED = 1e30
LOWEST = -3.0e38
RSQRT_SEED = float(0x5f3759df - (1 << 22) - (1 << 31))
NEWTON_STEPS = 3


def gat_moe_kernel(nc, x, adj, W1, a_src1, a_dst1, b1, W2, a_src2, a_dst2, b2, router_w, w1, w2, w3, out):
    B, N, D = x.shape
    H, FH = a_src1.shape
    HF = H * FH
    E, _, F = w1.shape
    NJ = N // P
    KD = D // P
    KF = HF // P
    FT = F // P
    BLK = 512
    SB_B = 4
    SB_T = SB_B * N
    NBLK = SB_T // BLK
    TT = BLK // P
    NSB = B // SB_B
    EI = E // SB_B
    UNITS = EI * NBLK * FT
    WC = KD * F
    W2N = D + 2
    assert N == 256 and D == 256 and FH == P and WC == FT * D == 1024 and NSB % 2 == 0

    with ExitStack() as ctx:
        def sb(name, shape, dt):
            return ctx.enter_context(nc.sbuf_tensor(name, shape, dt))

        def sem(name):
            return ctx.enter_context(nc.semaphore(name))

        ident = sb("ident", [P, P], F32)
        ident_r = sb("ident_r", [P, P], F32R)
        ident_b = sb("ident_b", [P, P], BF16)
        eye = sb("eye", [P, NJ, N], BF16)
        head_row = sb("head_row", [2 * H, H, P], F32R)
        expert_id = sb("expert_id", [P, E], F32)
        W1s = [sb(f"W1_{s}", [P, KD, HF], F32R) for s in "hl"]
        W2s = [sb(f"W2_{s}", [P, KF, W2N], F32R) for s in "hl"]
        v1s = [sb(f"v1_{s}", [P, KD, P], F32R) for s in "hl"]
        rws = [sb(f"rw_{s}", [P, KD, P], F32R) for s in "hl"]
        v2f = sb("v2f", [P, KF, 2], F32)
        b1T = sb("b1T", [P, H], F32)
        b2b = sb("b2b", [P, D], F32)

        stage = sb("stage", [P, 2, WC], F32)
        we1 = [[sb(f"we1_{e}{s}", [P, KD, F], F32R) for s in "hl"] for e in range(EI)]
        we3 = [[sb(f"we3_{e}{s}", [P, KD, F], F32R) for s in "hl"] for e in range(EI)]
        we2 = [[sb(f"we2_{e}{s}", [P, FT, D], F32R) for s in "hl"] for e in range(EI)]

        xTs = [sb(f"xT_{s}", [P, KD, 2 * SB_T], F32R) for s in "hl"]
        yacc = sb("yacc", [P, 2 * SB_B * NJ, D], F32)
        comb = sb("comb", [P, 2 * SB_B * NJ, E], F32)
        cw = sb("cw", [P, SB_B * NJ, EI], F32)
        hb = sb("hb", [P, 2, BLK], F32)
        hhs = [sb(f"hh_{s}", [P, 2, BLK], F32R) for s in "hl"]

        xb = sb("xb", [P, NJ, D], F32)
        adjb = sb("adjb", [P, NJ, N], I32)
        xn = sb("xn", [P, NJ, D], F32)
        mask = sb("mask", [P, NJ, N], BF16)
        mbias = sb("mbias", [P, NJ, N], F32)
        nTs = [sb(f"nT_{s}", [P, KD, N], F32R) for s in "hl"]
        rows_f = sb("rows_f", [2 * H, N], F32)
        rows_s = [sb(f"rows_{s}", [2 * H, N], F32R) for s in "hl"]
        lrows = sb("lrows", [E, N], F32)
        cols = sb("cols", [P, NJ, 2 * H], F32)
        xls = [sb(f"xl_{s}", [P, NJ, HF], F32R) for s in "hl"]
        sc = sb("sc", [P, 2, NJ, N], F32)
        e1 = sb("e1", [P, H, NJ, N], F32)
        e2 = sb("e2", [P, 2, NJ, N], F32)
        PTs = [sb(f"PT_{s}", [P, 2, NJ, N], F32R) for s in "hl"]
        z = sb("z", [P, H, N], F32)
        h1s = [sb(f"h1_{s}", [P, KF, N], F32R) for s in "hl"]
        a2c = sb("a2c", [P, NJ, 2], F32)
        a2s = [sb(f"a2_{s}", [P, NJ, P], F32R) for s in "hl"]
        st = sb("st", [P, NJ, 6], F32)
        mv = sb("mv", [P, NJ, 2], F32)
        nw = sb("nw", [P, 4, NJ], F32)
        mx = sb("mx", [P, NJ, 2], F32)
        mm_ = sb("mm_", [P, NJ, 2], F32)
        bi1 = sb("bi1", [P, NJ, 2], F32)
        bi2 = sb("bi2", [P, NJ, 2], F32)
        sm = sb("sm", [P, NJ, 2], F32)
        rs = sb("rs", [P, NJ, 2], F32)
        lg = sb("lg", [P, NJ, E], F32)
        top = sb("top", [P, NJ, 8], F32)
        topi = sb("topi", [P, NJ, 8], U32)
        topf = sb("topf", [P, NJ, 8], F32)
        gap = sb("gap", [P, NJ], F32)
        eg = sb("eg", [P, NJ], F32)
        wts = sb("wts", [P, 3, NJ], F32)
        oh = sb("oh", [P, 2, NJ, E], F32)

        pG = [ctx.enter_context(nc.psum_tensor(f"pG{i}", [P, BLK], F32)) for i in range(2)]
        pU = [ctx.enter_context(nc.psum_tensor(f"pU{i}", [P, BLK], F32)) for i in range(2)]
        pY = [ctx.enter_context(nc.psum_tensor(f"pY{i}", [P, 2, D], F32)) for i in range(2)]
        pA = ctx.enter_context(nc.psum_tensor("pA", [P, 512], F32))
        pB = ctx.enter_context(nc.psum_tensor("pB", [P, 512], F32))

        maskT = pB[:, 0:NJ * N // 2].bitcast(BF16)
        bank_PT = [pA, pB, pB, pA, pB]
        bank_A1 = [pA, pB]
        bank_X2 = [pA, pB]

        def flat(t_):
            return t_[:, :, :].rearrange("p a b -> p (a b)")

        def fold(t_, n=2):
            return t_[:, :].rearrange("p (a b) -> p a b", a=n)

        s_cin = sem("const_loaded")
        s_w12 = sem("gat_weights_loaded")
        s_cz = sem("const_zeroed")
        s_cid = sem("const_built")
        s_cr = sem("const_rounded")
        s_prep = sem("prep_order")
        s_prepd = sem("prep_done")
        s_x = sem("x_loaded")
        s_adj = sem("adj_loaded")
        s_xb2 = sem("bias2_added")
        s_maskp = sem("mask_marks_2_per_graph")
        s_mask = sem("mask_ready")
        s_dg = sem("dve_graph_order")
        s_norm = sem("dve_norm_order")
        s_ln1 = sem("ln1_ready")
        s_T1 = sem("T1_done")
        s_nTh = sem("nT_high")
        s_nT = sem("nT_ready")
        s_MT = sem("mask_transposed")
        s_mb = sem("mask_bias_ready")
        s_RW = sem("score_rows_done")
        s_rwc = sem("score_rows_copied")
        s_rwl = sem("score_rows_low")
        s_CT = sem("score_cols_done")
        s_cols = sem("score_cols_copied")
        s_X1 = sem("features1_done_2_per_graph")
        s_xlh = sem("features1_high_2_per_graph")
        s_xll = sem("features1_low_2_per_graph")
        s_SB = sem("source_scores_spread_2_per_graph")
        s_max = sem("score_bias_ready_3_per_graph")
        s_exp = sem("exps_done_3_per_graph")
        s_pn = sem("probs_ready_3_per_graph")
        s_PT = sem("probs_transposed_5_per_graph")
        s_PTh = sem("probsT_high_5_per_graph")
        s_PTl = sem("probsT_low_5_per_graph")
        s_A1 = sem("attended1_done_4_per_graph")
        s_z = sem("attended1_biased_2_per_graph")
        s_zn = sem("elu_negative_part_2_per_graph")
        s_ze = sem("elu_exp_2_per_graph")
        s_zf = sem("elu_done_2_per_graph")
        s_h1h = sem("h1_high_2_per_graph")
        s_h1 = sem("h1_ready_2_per_graph")
        s_X2 = sem("features2_done_2_per_graph")
        s_x2h = sem("features2_high_2_per_graph")
        s_x2l = sem("features2_low_2_per_graph")
        s_a2 = sem("source2_columns_ready")
        s_B2 = sem("source2_scores_spread")
        s_A2 = sem("attended2_done")
        s_x1 = sem("gnn_residual_ready")
        s_ln2 = sem("ln2_ready")
        s_T2 = sem("T2_done")
        s_fTh = sem("ffn_xT_high")
        s_fT = sem("ffn_xT_ready")
        s_RT = sem("router_rows_done")
        s_lr = sem("router_rows_copied")
        s_LC = sem("router_cols_done")
        s_lg = sem("router_cols_copied")
        s_gap = sem("logit_gap_ready")
        s_eg = sem("gap_exp_done")
        s_comb = sem("combine_ready")
        s_wst = [sem("chunk_loaded_0"), sem("chunk_loaded_1")]
        s_wh = sem("chunk_high")
        s_wl = sem("chunk_split")
        s_g = sem("gate_done")
        s_u = sem("up_done")
        s_th = sem("tanh_done")
        s_a = sem("gate_used")
        s_h = sem("hidden_ready")
        s_hh = sem("hidden_high")
        s_hl = sem("hidden_low")
        s_dn = sem("down_done")
        s_cw = sem("weights_of_pair_ready")
        s_y = sem("y_added")
        s_out = sem("out_stored")

        CREDIT = 2
        START = 1
        LAG = 2
        GROUPS = EI * NBLK
        NORM_LINKS = 5 + 2 * NEWTON_STEPS
        DVE_LINKS = 23
        NW = 3
        NWI = NW * EI

        block = ctx.enter_context(nc.Block())

        def run_iterations(eng, graph_only, ffn):
            with eng.Fori(0, SB_B) as p:
                graph_only(p, p, 0)
            ffn(0, 0, 0, first=True)
            with eng.Fori(0, NSB // 2 - 1) as s2:
                with eng.Fori(1, SB_B) as p:
                    ffn(s2 * (2 * SB_B), p, 0)
                with eng.Fori(0, SB_B) as p:
                    ffn(s2 * (2 * SB_B) + SB_B, p, 1)
                ffn(s2 * (2 * SB_B) + 2 * SB_B, 0, 0)
            with eng.Fori(1, SB_B - 1) as p:
                ffn(B - 2 * SB_B, p, 0)
            ffn(B - 2 * SB_B, SB_B - 1, 0, ahead=False)
            with eng.Fori(0, SB_B - 1) as p:
                ffn(B - SB_B, p, 1, graph=False)
            ffn(B - SB_B, SB_B - 1, 1, graph=False, last=True)

        def wait_alone(eng, *waits):
            counts = [(s, v if isinstance(v, int) else eng.to_reg(v)) for s, v in waits]
            eng.wait_ge(s_prepd, 1)
            for s, v in counts:
                eng.wait_ge(s, v)

        @block.sync
        def _(sp):
            for n, a in enumerate((a_src1, a_dst1)):
                sp.dma_start(hb[:, n, :], a.rearrange("(o h) f -> o (h f)", o=1).broadcast_to([P, HF])).then_inc(s_cin, 16)
            for n, a in enumerate((a_src2, a_dst2)):
                sp.dma_start(e2[:, 0, n, :], a.broadcast_to([P, D])).then_inc(s_cin, 16)
            sp.dma_start(b2b[:, :], b2.rearrange("(o d) -> o d", o=1).broadcast_to([P, D])).then_inc(s_cin, 16)
            sp.dma_start(b1T[:, :], b1.rearrange("(h f) -> f h", f=P), allow_slow_non_contiguous=True).then_inc(s_cin, 16)
            sp.dma_start(stage[:, 0, :].rearrange("p (k n) -> p k n", k=KD), W1.rearrange("(k p) n -> p k n", p=P)).then_inc(s_w12, 16)
            sp.dma_start(stage[:, 1, :].rearrange("p (k n) -> p k n", k=KF), W2.rearrange("(k p) n -> p k n", p=P)).then_inc(s_w12, 16)
            sp.wait_ge(s_cz, 1)
            sp.dma_start(z[:, 0:KD, P:P + E], router_w.rearrange("(k p) e -> p k e", p=P)).then_inc(s_cin, 16)

            def load_graph(b, first=False):
                if not first:
                    sp.wait_ge(s_x1, b)
                sp.dma_start(xb[:, :, :], x[bass.ds(b, 1)].rearrange("o (j p) d -> p (o j) d", p=P)).then_inc(s_x, 16)
                if not first:
                    sp.wait_ge(s_maskp, 2 * b)
                sp.dma_start(adjb[:, :, :], adj[bass.ds(b, 1)].rearrange("o (j p) d -> p (o j) d", p=P)).then_inc(s_adj, 16)

            def load_chunk(e, c, n, first=False):
                slot = (e * NW + c) % 2
                if not first:
                    sp.wait_ge(s_wl, n - 1)
                else:
                    sp.wait_ge(s_prepd, 1)
                dst = stage[:, slot, :].rearrange("p (k n) -> p k n", k=KD if c < 2 else FT)
                src = (w1, w3, w2)[c][e].rearrange("(k p) n -> p k n", p=P)
                sp.dma_start(dst, src).then_inc(s_wst[slot], 16)

            def load_expert(e, n0, first=False):
                for c in range(NW):
                    load_chunk(e, c, n0 + c, first and c < 2)

            sp.sem_inc(s_out, START)
            load_graph(0, True)
            load_expert(0, 0, True)
            with sp.Fori(1, SB_B + 1) as b:
                load_graph(b)

            def store(s, par):
                sp.wait_ge(s_y, START + NBLK * E * (s + 1))
                sp.dma_start(out[bass.ds(s * SB_B, SB_B)].rearrange("g (j p) d -> p (g j) d", p=P),
                             yacc[:, par * SB_B * NJ:(par + 1) * SB_B * NJ, :]).then_inc(s_out, 16)

            def iteration(s, q, last_sb=False, ahead=True):
                if q > 0:
                    load_expert(EI * q + 1, s * NW * E + NW * (EI * q + 1))
                if not (last_sb and q == SB_B - 1):
                    load_expert((EI * q + EI) % E, s * NW * E + NW * (EI * q + EI))
                if ahead:
                    load_graph(s * SB_B + q + SB_B + 1)

            load_expert(1, NW)
            with sp.Fori(0, NSB // 2 - 1) as sh:
                for par in range(2):
                    s = sh * 2 + par
                    for q in range(SB_B):
                        iteration(s, q)
                    load_expert(1, (s + 1) * NW * E + NW)
                    store(s, par)
            for q in range(SB_B):
                iteration(NSB - 2, q, ahead=q < SB_B - 1)
            load_expert(1, (NSB - 1) * NW * E + NW)
            store(NSB - 2, 0)
            for q in range(SB_B):
                iteration(NSB - 1, q, last_sb=True, ahead=False)
            store(NSB - 1, 1)
            sp.wait_ge(s_out, START + 16 * NSB)

        PHASES = 3 * UNITS
        PE_AT = dict(T1=1, MT=4, RW=3, X1_0=5, CT=6, X1_1=7, SB0=7, SB1=8, PT0=14, PT1=15, A1_0=17, A1_1=18, PT2=20,
                     PT3=22, A1_2=24, A1_3=24, X2_0=29, X2_1=30, B2=32, PT4=36, A2=38, T2=41, RT=43, LC=45)
        ACT_AT = dict(T1_high=1, mask_bias=4, rows=3, X1_high0=5, X1_high1=7, exp0=9, PT_high0=14, PT_high1=15,
                      exp1=15, bias0=18, elu_exp0=18, PT_high2=20, PT_high3=22, bias1=25, elu_exp1=25, h1_high0=26,
                      h1_high1=26, X2_high0=29, X2_high1=30, exp2=33, PT_high4=36, T2_high=41, RT_rows=43, gap_exp=46)
        DVE_AT = dict(T1_low=1, rows_low=3, X1_low0=5, cols=6, X1_low1=7, max0=8, prob0=10, max1=11, PT_low0=14,
                      PT_low1=15, elu_neg0=18, prob1=18, PT_low2=20, elu_sum0=20, PT_low3=22, elu_neg1=25,
                      elu_sum1=26, X2_low0=29, X2_low1=30, source2=30, max2=32, prob2=34, PT_low4=36, x1=38, norm2=38,
                      T2_low=41, top=46, comb=47, norm1_next=44)
        POOL_AT = dict(mask=0, bias2=3, h1_low0=24, h1_low1=24)

        @block.gpsimd
        def _(pool):
            nc.gpsimd.memset(ident[:, :], 0.0)
            nc.gpsimd.memset(eye[:, :, :], 0.0)
            nc.gpsimd.memset(z[:, :, :], 0.0).then_inc(s_cz, 1)
            for e in range(E):
                nc.gpsimd.memset(expert_id[:, e:e + 1], float(e))
            pool.wait_ge(s_cz, 1)
            nc.gpsimd.affine_select(out=ident[:, :], in_=ident[:, :], compare_op=ALU.not_equal, fill=1.0, base=0,
                                    pattern=[[-1, P]], channel_multiplier=1)
            nc.gpsimd.affine_select(out=eye[:, :, :], in_=eye[:, :, :], compare_op=ALU.not_equal, fill=1.0, base=0,
                                    pattern=[[P, NJ], [-1, N]], channel_multiplier=1)
            spread = z[0:2 * H, 0:H, 0:P]
            nc.gpsimd.affine_select(out=spread, in_=spread, compare_op=ALU.not_equal, fill=1.0, base=0,
                                    pattern=[[-1, H], [0, P]], channel_multiplier=1).then_inc(s_cid, 1)
            pool.wait_ge(s_cid, 1)
            nc.gpsimd.tensor_copy(ident_r[:, :], ident[:, :])
            nc.gpsimd.tensor_copy(ident_b[:, :], ident[:, :])
            nc.gpsimd.tensor_copy(head_row[:, :, :], spread).then_inc(s_cr, 1)
            pool.sem_inc(s_hl, CREDIT)
            pool.sem_inc(s_h1, START)

            def chunk_low(el, c, i, ahead):
                k = NW * el + c
                dh, dl = (flat((we1, we3, we2)[c][el][s]) for s in range(2))
                pool.wait_ge(s_wh, NWI * (i + ahead) + k + 1)
                nc.gpsimd.tensor_tensor(dl, stage[:, k % 2, :], dh, ALU.subtract).then_inc(s_wl, 1)

            def graph_inputs(b):
                wait_alone(pool, (s_adj, 16 * b + 16), (s_MT, START + b))
                nc.gpsimd.tensor_scalar(mask[:, :, :], adjb[:, :, :], 0.0, None, ALU.is_gt).then_inc(s_maskp, 1)
                pool.wait_ge(s_maskp, 2 * b + 1)
                nc.gpsimd.tensor_tensor(mask[:, :, :], mask[:, :, :], eye[:, :, :], ALU.add).then_inc(s_maskp, 1)
                wait_alone(pool, (s_maskp, 2 * b + 2))
                nc.gpsimd.tensor_scalar(mask[:, :, :], mask[:, :, :], 1.0, None, ALU.min).then_inc(s_mask, 1)

            def graph_bias(b):
                pool.wait_ge(s_ln1, b + 1)
                nc.gpsimd.tensor_tensor(xb[:, :, :], xb[:, :, :], b2b[:, :].unsqueeze(1).broadcast_to([P, NJ, D]),
                                        ALU.add).then_inc(s_xb2, 1)

            def graph_h1_low(b, g):
                pool.wait_ge(s_h1h, 2 * b + g + 1)
                hs = slice(2 * g, 2 * g + 2)
                nc.gpsimd.tensor_tensor(h1s[1][:, hs, :], z[:, hs, :], h1s[0][:, hs, :], ALU.subtract).then_inc(s_h1, 1)

            def graph_phase(b, ph):
                if ph == POOL_AT["mask"]:
                    graph_inputs(b)
                if ph == POOL_AT["bias2"]:
                    graph_bias(b)
                if ph == POOL_AT["h1_low0"]:
                    graph_h1_low(b, 0)
                if ph == POOL_AT["h1_low1"]:
                    graph_h1_low(b, 1)

            def hidden_low(i, u):
                pool.wait_ge(s_hh, UNITS * i + u + 1)
                nc.gpsimd.tensor_tensor(hhs[1][:, u % 2, :], hb[:, u % 2, :], hhs[0][:, u % 2, :],
                                        ALU.subtract).then_inc(s_hl, 1)

            def graph_only(b, p, par):
                for ph in range(PHASES):
                    graph_phase(b, ph)

            def ffn(base, p, par, graph=True, ahead=True, first=False, last=False):
                i = base + p
                half = UNITS // 2
                for u in range(UNITS):
                    if graph:
                        graph_phase(i + SB_B, 3 * u)
                    if u == LAG:
                        pool.wait_ge(s_dn, UNITS * i + CREDIT)
                    if LAG <= u < LAG + NW:
                        chunk_low(1, u - LAG, i, 0)
                    hidden_low(i, u)
                    if u == half + 2:
                        pool.wait_ge(s_dn, UNITS * i + half + CREDIT)
                    if half + 2 <= u < half + 2 + NW and not last:
                        chunk_low(0, u - half - 2, i, 1)
                    if graph:
                        graph_phase(i + SB_B, 3 * u + 1)
                        graph_phase(i + SB_B, 3 * u + 2)

            pool.wait_ge(s_prepd, 1)
            for c in range(NW):
                chunk_low(0, c, 0, 0)
            run_iterations(pool, graph_only, ffn)

        @block.scalar
        def _(act):
            def nT_high(b):
                act.wait_ge(s_T1, b + 1)
                act.wait_ge(s_A2, START + b)
                nc.scalar.activation(flat(nTs[0]), pA[:, :], ACT.Copy).then_inc(s_nTh, 1)

            def mask_bias(b):
                act.wait_ge(s_MT, START + b + 1)
                act.wait_ge(s_max, START + 3 * b)
                nc.scalar.activation(flat(mbias), maskT, ACT.Copy, bias=-MASKED, scale=MASKED).then_inc(s_mb, 1)

            def rows_copy(b):
                act.wait_ge(s_RW, b + 1)
                act.wait_ge(s_SB, START + 2 * b)
                nc.scalar.activation(rows_f[:, :], pA[0:2 * H, 0:N], ACT.Copy)
                nc.scalar.activation(rows_s[0][:, :], pA[0:2 * H, 0:N], ACT.Copy).then_inc(s_rwc, 1)

            def features1_high(b, j):
                act.wait_ge(s_X1, 2 * b + j + 1)
                act.wait_ge(s_A1, START + H * b)
                nc.scalar.activation(xls[0][:, j, :], pB[:, :], ACT.Copy).then_inc(s_xlh, 1)

            def exps(b, g):
                act.wait_ge(s_max, START + 3 * b + g + 1)
                if g != 1:
                    act.wait_ge(s_PT, START + (H + 1) * b + g)
                if g > 0:
                    act.wait_ge(s_pn, 3 * b + g)
                for h in range(2 if g < 2 else 1):
                    for j in range(NJ):
                        nc.scalar.activation(e1[:, 2 * (g % 2) + h, j, :], sc[:, h, j, :], ACT.Exp, bias=bi1[:, j, h:h + 1])
                        last = nc.scalar.activation(e2[:, h, j, :], sc[:, h, j, :], ACT.Exp, bias=bi2[:, j, h:h + 1],
                                                    scale=NEG_SLOPE)
                last.then_inc(s_exp, 1)

            def probs_high(b, h):
                act.wait_ge(s_PT, START + (H + 1) * b + h + 1)
                if h == 0:
                    act.wait_ge(s_A2, START + b)
                else:
                    act.wait_ge(s_A1, START + H * b + max(h - 1, 0))
                nc.scalar.activation(PTs[0][:, h % 2, :, :].rearrange("p j n -> p (j n)"), bank_PT[h][:, :],
                                     ACT.Copy).then_inc(s_PTh, 1)

            def attended_bias(b, g):
                act.wait_ge(s_A1, START + H * b + 2 * g + 2)
                act.wait_ge(s_h1, START + 2 * b)
                for h in range(2):
                    last = nc.scalar.activation(z[:, 2 * g + h, :], bank_A1[g][:, h * N:(h + 1) * N], ACT.Identity,
                                                bias=b1T[:, 2 * g + h:2 * g + h + 1])
                last.then_inc(s_z, 1)

            def elu_exp(b, g):
                act.wait_ge(s_zn, 2 * b + g + 1)
                nc.scalar.activation(xn[:, :, :], xn[:, :, :], ACT.Exp).then_inc(s_ze, 1)

            def h1_high(b, g):
                act.wait_ge(s_zf, 2 * b + g + 1)
                act.wait_ge(s_X2, START + 2 * b)
                nc.scalar.activation(h1s[0][:, 2 * g:2 * g + 2, :], z[:, 2 * g:2 * g + 2, :], ACT.Copy).then_inc(s_h1h, 1)

            def features2_high(b, j):
                act.wait_ge(s_X2, START + 2 * b + j + 1)
                nc.scalar.activation(nTs[0][:, j, :], bank_X2[j][:, 0:D], ACT.Copy).then_inc(s_x2h, 1)

            def ffn_x_high(b, p, par):
                act.wait_ge(s_T2, b + 1)
                nc.scalar.activation(xTs[0][:, :, bass.ds(p * N + par * SB_T, N)], fold(pB), ACT.Copy).then_inc(s_fTh, 1)

            def router_rows(b):
                act.wait_ge(s_RT, b + 1)
                nc.scalar.activation(lrows[:, :], pA[0:E, 0:N], ACT.Copy).then_inc(s_lr, 1)

            def gap_exp(b):
                act.wait_ge(s_gap, b + 1)
                nc.scalar.activation(eg[:, :], gap[:, :], ACT.Exp).then_inc(s_eg, 1)

            def graph_phase(b, p, par, ph):
                if ph == ACT_AT["T1_high"]:
                    nT_high(b)
                if ph == ACT_AT["mask_bias"]:
                    mask_bias(b)
                if ph == ACT_AT["rows"]:
                    rows_copy(b)
                if ph == ACT_AT["X1_high0"]:
                    features1_high(b, 0)
                if ph == ACT_AT["X1_high1"]:
                    features1_high(b, 1)
                if ph == ACT_AT["exp0"]:
                    exps(b, 0)
                if ph == ACT_AT["PT_high0"]:
                    probs_high(b, 0)
                if ph == ACT_AT["PT_high1"]:
                    probs_high(b, 1)
                if ph == ACT_AT["exp1"]:
                    exps(b, 1)
                if ph == ACT_AT["bias0"]:
                    attended_bias(b, 0)
                if ph == ACT_AT["elu_exp0"]:
                    elu_exp(b, 0)
                if ph == ACT_AT["PT_high2"]:
                    probs_high(b, 2)
                if ph == ACT_AT["PT_high3"]:
                    probs_high(b, 3)
                if ph == ACT_AT["bias1"]:
                    attended_bias(b, 1)
                if ph == ACT_AT["elu_exp1"]:
                    elu_exp(b, 1)
                if ph == ACT_AT["h1_high0"]:
                    h1_high(b, 0)
                if ph == ACT_AT["h1_high1"]:
                    h1_high(b, 1)
                if ph == ACT_AT["X2_high0"]:
                    features2_high(b, 0)
                if ph == ACT_AT["X2_high1"]:
                    features2_high(b, 1)
                if ph == ACT_AT["exp2"]:
                    exps(b, 2)
                if ph == ACT_AT["PT_high4"]:
                    probs_high(b, H)
                if ph == ACT_AT["T2_high"]:
                    ffn_x_high(b, p, par)
                if ph == ACT_AT["RT_rows"]:
                    router_rows(b)
                if ph == ACT_AT["gap_exp"]:
                    gap_exp(b)

            def chunk_high(el, c, i, ahead):
                k = NW * el + c
                act.wait_ge(s_wst[k % 2], 8 * NWI * (i + ahead) + 16 * (k // 2) + 16)
                nc.scalar.activation(flat((we1, we3, we2)[c][el][0]), stage[:, k % 2, :], ACT.Copy).then_inc(s_wh, 1)

            def gate_tanh(i, u):
                act.wait_ge(s_g, UNITS * i + u + 1)
                act.wait_ge(s_hl, UNITS * i + u + 1)
                nc.scalar.activation(hb[:, u % 2, :], pG[u % 2][:, :], ACT.Tanh, scale=0.5).then_inc(s_th, 1)

            def hidden_high(i, u):
                act.wait_ge(s_h, UNITS * i + u + 1 + CREDIT)
                act.wait_ge(s_dn, UNITS * i + u + 1)
                nc.scalar.activation(hhs[0][:, u % 2, :], hb[:, u % 2, :], ACT.Copy).then_inc(s_hh, 1)

            def graph_only(b, p, par):
                for ph in range(PHASES):
                    graph_phase(b, p, par, ph)

            def ffn(base, p, par, graph=True, ahead=True, first=False, last=False):
                i = base + p
                half = UNITS // 2
                for u in range(UNITS):
                    gate_tanh(i, u)
                    if graph:
                        graph_phase(i + SB_B, p, 1 - par, 3 * u)
                        graph_phase(i + SB_B, p, 1 - par, 3 * u + 1)
                    hidden_high(i, u)
                    if u == LAG:
                        act.wait_ge(s_dn, UNITS * i + CREDIT)
                    if LAG <= u < LAG + NW:
                        chunk_high(1, u - LAG, i, 0)
                    if u == half + 2:
                        act.wait_ge(s_dn, UNITS * i + half + CREDIT)
                    if half + 2 <= u < half + 2 + NW and not last:
                        chunk_high(0, u - half - 2, i, 1)
                    if graph:
                        graph_phase(i + SB_B, p, 1 - par, 3 * u + 2)

            act.sem_inc(s_exp, START)
            act.sem_inc(s_lr, START)
            act.wait_ge(s_prepd, 1)
            for c in range(NW):
                chunk_high(0, c, 0, 0)
            run_iterations(act, graph_only, ffn)

        @block.vector
        def _(dve):
            prepared = [0]

            def prep(ins):
                prepared[0] += 1
                ins.then_inc(s_prep, 1)
                dve.wait_ge(s_prep, prepared[0])

            dve.wait_ge(s_w12, 32)
            dve.wait_ge(s_cz, 1)
            dve.wait_ge(s_cin, 16 * 7)
            nc.vector.tensor_copy(flat(W1s[0]), stage[:, 0, :])
            prep(nc.vector.tensor_copy(W2s[0][:, :, 0:D], fold(stage[:, 1, :], KF)))
            nc.vector.tensor_tensor(flat(W1s[1]), stage[:, 0, :], flat(W1s[0]), ALU.subtract)
            nc.vector.tensor_tensor(W2s[1][:, :, 0:D], fold(stage[:, 1, :], KF), W2s[0][:, :, 0:D], ALU.subtract)
            tmp = sc[:, :, :, :].rearrange("p a j n -> p (a j n)")
            for k in range(KD):
                for n in range(2):
                    prep(nc.vector.tensor_tensor(tmp[:, 0:HF], stage[:, 0, k * HF:(k + 1) * HF], hb[:, n, :], ALU.mult))
                    prep(nc.vector.tensor_reduce(z[:, KD + k, P + n * H:P + (n + 1) * H],
                                                 tmp[:, 0:HF].rearrange("p (h f) -> p h f", h=H), AX_X, ALU.add))
            for n in range(2):
                w = tmp[:, 0:KF * D].rearrange("p (k n) -> p k n", k=KF)
                prep(nc.vector.tensor_tensor(w, fold(stage[:, 1, :], KF),
                                             e2[:, 0, n, :].unsqueeze(1).broadcast_to([P, KF, D]), ALU.mult))
                prep(nc.vector.tensor_reduce(v2f[:, :, n], w, AX_X, ALU.add))
            nc.vector.tensor_copy(rws[0][:, :, :], z[:, 0:KD, P:2 * P])
            nc.vector.tensor_copy(v1s[0][:, :, :], z[:, KD:2 * KD, P:2 * P])
            prep(nc.vector.tensor_copy(W2s[0][:, :, D:W2N], v2f[:, :, :]))
            nc.vector.tensor_tensor(rws[1][:, :, :], z[:, 0:KD, P:2 * P], rws[0][:, :, :], ALU.subtract)
            nc.vector.tensor_tensor(v1s[1][:, :, :], z[:, KD:2 * KD, P:2 * P], v1s[0][:, :, :], ALU.subtract)
            nc.vector.tensor_tensor(W2s[1][:, :, D:W2N], v2f[:, :, :], W2s[0][:, :, D:W2N],
                                    ALU.subtract).then_inc(s_prepd, 1)
            dve.sem_inc(s_a, CREDIT)
            dve.sem_inc(s_h, CREDIT)
            for s_ in (s_max, s_lg, s_y):
                dve.sem_inc(s_, START)

            links = [0]

            def link(ins, b, alone=False):
                links[0] += 1
                ins.then_inc(s_dg, 1)
                if alone:
                    wait_alone(dve, (s_dg, DVE_LINKS * b + links[0]))
                else:
                    dve.wait_ge(s_dg, DVE_LINKS * b + links[0])

            def layer_norm(b, which, rows, done):
                at = [NORM_LINKS * (2 * b + which), 0]

                def then(ins):
                    at[1] += 1
                    ins.then_inc(s_norm, 1)
                    if at[1] == 1:
                        wait_alone(dve, (s_norm, at[0] + at[1]))
                    else:
                        dve.wait_ge(s_norm, at[0] + at[1])

                for j in range(NJ):
                    last = nc.vector.bn_stats(st[:, j, :], rows[j])
                then(last)
                for j in range(NJ):
                    last = nc.vector.bn_aggr(mv[:, j, :], st[:, j, :])
                then(last)
                h, y, s = (nw[:, k, :] for k in range(3))
                then(nc.vector.tensor_scalar(h, mv[:, :, 1], LN_EPS, 0.5, ALU.add, ALU.mult))
                then(nc.vector.tensor_scalar(s.bitcast(I32), h.bitcast(I32), 1, None, ALU.arith_shift_right))
                then(nc.vector.tensor_scalar(y.bitcast(I32), s.bitcast(I32), -1.0, RSQRT_SEED, ALU.mult, ALU.add))
                for _ in range(NEWTON_STEPS):
                    for j in range(NJ):
                        last = nc.vector.tensor_scalar(s[:, j:j + 1], y[:, j:j + 1], y[:, j:j + 1], h[:, j:j + 1],
                                                       ALU.mult, ALU.mult)
                    then(last)
                    then(nc.vector.scalar_tensor_tensor(y, s, -1.5, y, ALU.add, ALU.mult))
                assert at[1] == NORM_LINKS
                for j in range(NJ):
                    last = nc.vector.tensor_scalar(xn[:, j, :], rows[j], mv[:, j, 0:1], y[:, j:j + 1],
                                                   ALU.subtract, ALU.mult)
                last.then_inc(done, 1)

            def norm1(b):
                dve.wait_ge(s_x, 16 * b + 16)
                layer_norm(b, 0, [xb[:, j, :] for j in range(NJ)], s_ln1)

            def nT_low(b):
                dve.wait_ge(s_nTh, b + 1)
                nc.vector.tensor_tensor(flat(nTs[1]), pA[:, :], flat(nTs[0]), ALU.subtract).then_inc(s_nT, 1)

            def rows_low(b):
                dve.wait_ge(s_rwc, b + 1)
                nc.vector.tensor_tensor(rows_s[1][:, :], pA[0:2 * H, 0:N], rows_s[0][:, :], ALU.subtract).then_inc(s_rwl, 1)

            def cols_copy(b):
                dve.wait_ge(s_CT, b + 1)
                nc.vector.tensor_copy(flat(cols), pA[:, 0:NJ * 2 * H]).then_inc(s_cols, 1)

            def features1_low(b, j):
                dve.wait_ge(s_xlh, 2 * b + j + 1)
                nc.vector.tensor_tensor(xls[1][:, j, :], pB[:, :], xls[0][:, j, :], ALU.subtract).then_inc(s_xll, 1)

            def softmax_max(b, g):
                exps_done = (s_exp, START + 3 * b + g)
                if g < 2:
                    wait_alone(dve, exps_done, (s_SB, START + 2 * b + g + 1), (s_mb, b + 1), (s_cols, b + 1))
                    spread, target, nh = (pA, pB)[g], cols[:, :, H + 2 * g:H + 2 * g + 2], 2
                else:
                    wait_alone(dve, exps_done, (s_B2, b + 1))
                    spread, target, nh = pA, a2c[:, :, 1:2], 1
                for h in range(nh):
                    for j in range(NJ):
                        last = nc.vector.tensor_tensor_reduce(sc[:, h, j, :], spread[:, h * N:(h + 1) * N], mbias[:, j, :],
                                                              1.0, LOWEST, ALU.add, ALU.max, mx[:, j, h:h + 1])
                link(last, b)
                m, mt = mm_[:, :, 0:nh], mx[:, :, 0:nh]
                link(nc.vector.tensor_tensor(mt, mt, target, ALU.add), b)
                link(nc.vector.scalar_tensor_tensor(m, mt, NEG_SLOPE, mt, ALU.mult, ALU.max), b)
                nc.vector.tensor_tensor(bi1[:, :, 0:nh], target, m, ALU.subtract)
                nc.vector.scalar_tensor_tensor(bi2[:, :, 0:nh], target, NEG_SLOPE, m, ALU.mult,
                                               ALU.subtract).then_inc(s_max, 1)

            def softmax_probs(b, g):
                dve.wait_ge(s_exp, START + 3 * b + g + 1)
                nh = 2 if g < 2 else 1
                for h in range(nh):
                    for j in range(NJ):
                        e = e1[:, 2 * (g % 2) + h, j, :]
                        last = nc.vector.scalar_tensor_tensor(e, e, 1.0, e2[:, h, j, :], ALU.mult, ALU.max,
                                                              accum_out=sm[:, j, h:h + 1])
                if g == 2:
                    last.then_inc(s_pn, 1)
                    dve.wait_ge(s_pn, 3 * b + 3)
                    nc.vector.reciprocal(rs[:, :, 0:1], sm[:, :, 0:1])
                    return
                link(last, b)
                link(nc.vector.reciprocal(rs[:, :, :], sm[:, :, :]), b)
                for h in range(nh):
                    for j in range(NJ):
                        e = e1[:, 2 * (g % 2) + h, j, :]
                        last = nc.vector.tensor_scalar(e, e, rs[:, j, h:h + 1], None, ALU.mult)
                last.then_inc(s_pn, 1)

            def probs_low(b, h):
                dve.wait_ge(s_PTh, (H + 1) * b + h + 1)
                dst = (pt[:, h % 2, :, :].rearrange("p j n -> p (j n)") for pt in PTs)
                hi, lo = dst
                nc.vector.tensor_tensor(lo, bank_PT[h][:, :], hi, ALU.subtract).then_inc(s_PTl, 1)

            def elu_negative(b, g):
                dve.wait_ge(s_z, 2 * b + g + 1)
                if g == 1:
                    dve.wait_ge(s_zf, 2 * b + 1)
                zs, ts = z[:, 2 * g:2 * g + 2, :], xn[:, :, :]
                nc.vector.tensor_scalar(ts, zs, 0.0, None, ALU.min).then_inc(s_zn, 1)
                dve.wait_ge(s_zn, 2 * b + g + 1)
                link(nc.vector.tensor_scalar(zs, zs, 0.0, None, ALU.max), b)

            def elu_sum(b, g):
                dve.wait_ge(s_ze, 2 * b + g + 1)
                zs, ts = z[:, 2 * g:2 * g + 2, :], xn[:, :, :]
                nc.vector.scalar_tensor_tensor(zs.rearrange("p a b -> p (a b)"), ts.rearrange("p a b -> p (a b)"), -1.0,
                                               zs.rearrange("p a b -> p (a b)"), ALU.add, ALU.add).then_inc(s_zf, 1)

            def features2_low(b, j):
                dve.wait_ge(s_x2h, 2 * b + j + 1)
                nc.vector.tensor_copy(a2c[:, j, :], bank_X2[j][:, D:W2N])
                nc.vector.tensor_tensor(nTs[1][:, j, :], bank_X2[j][:, 0:D], nTs[0][:, j, :], ALU.subtract).then_inc(s_x2l, 1)

            def source2(b):
                dve.wait_ge(s_x2l, 2 * b + 2)
                src = a2c[:, :, 0:1].broadcast_to([P, NJ, P])
                link(nc.vector.tensor_copy(a2s[0][:, :, :], src), b)
                nc.vector.tensor_tensor(a2s[1][:, :, :], src, a2s[0][:, :, :], ALU.subtract).then_inc(s_a2, 1)

            def tokens(p, par, j):
                return bass.ds(p * NJ + par * SB_B * NJ + j, 1)

            def residual1(b, p, par, base):
                dve.wait_ge(s_A2, START + b + 1)
                dve.wait_ge(s_xb2, b + 1)
                if base is not None:
                    dve.wait_ge(s_out, START + base * (16 // SB_B))
                for j in range(NJ):
                    last = nc.vector.scalar_tensor_tensor(yacc[:, tokens(p, par, j), :], pA[:, j * D:(j + 1) * D],
                                                          rs[:, j, 0:1], xb[:, j, :], ALU.mult, ALU.add)
                last.then_inc(s_x1, 1)

            def ffn_x_low(b, p, par):
                dve.wait_ge(s_fTh, b + 1)
                at = bass.ds(p * N + par * SB_T, N)
                nc.vector.tensor_tensor(xTs[1][:, :, at], fold(pB), xTs[0][:, :, at], ALU.subtract).then_inc(s_fT, 1)

            def router_top(b):
                dve.wait_ge(s_LC, b + 1)
                nc.vector.tensor_copy(flat(lg), pB[:, 0:NJ * E]).then_inc(s_lg, 1)
                wait_alone(dve, (s_lg, START + b + 1))
                for j in range(NJ):
                    last = nc.vector.max(top[:, j, :], lg[:, j, :])
                link(last, b)
                nc.vector.tensor_tensor(gap[:, :], top[:, :, 1], top[:, :, 0], ALU.subtract).then_inc(s_gap, 1)
                for j in range(NJ):
                    last = nc.vector.max_index(topi[:, j, :], top[:, j, :], lg[:, j, :])
                link(last, b)
                link(nc.vector.tensor_copy(flat(topf), flat(topi)), b)

            def router_weights(b, p, par):
                dve.wait_ge(s_eg, b + 1)
                s, w0, w1_ = (wts[:, k, :] for k in range(3))
                link(nc.vector.tensor_scalar(s, eg[:, :], 2.0, 2.0, ALU.mult, ALU.add), b)
                link(nc.vector.reciprocal(w0, s), b)
                link(nc.vector.tensor_tensor(w1_, eg[:, :], w0, ALU.mult), b)
                for j in range(NJ):
                    for k, w in enumerate((w0, w1_)):
                        last = nc.vector.tensor_scalar(oh[:, k, j, :], expert_id[:, :], topf[:, j, k:k + 1], w[:, j:j + 1],
                                                       ALU.is_equal, ALU.mult)
                link(last, b)
                nc.vector.tensor_tensor(comb[:, bass.ds(p * NJ + par * SB_B * NJ, NJ), :], oh[:, 0, :, :], oh[:, 1, :, :],
                                        ALU.add).then_inc(s_comb, 1)

            def graph_phase(b, p, par, base, ph, ahead=True):
                if ph == DVE_AT["T1_low"]:
                    nT_low(b)
                if ph == DVE_AT["rows_low"]:
                    rows_low(b)
                if ph == DVE_AT["X1_low0"]:
                    features1_low(b, 0)
                if ph == DVE_AT["cols"]:
                    cols_copy(b)
                if ph == DVE_AT["X1_low1"]:
                    features1_low(b, 1)
                if ph == DVE_AT["max0"]:
                    softmax_max(b, 0)
                if ph == DVE_AT["prob0"]:
                    softmax_probs(b, 0)
                if ph == DVE_AT["max1"]:
                    softmax_max(b, 1)
                if ph == DVE_AT["PT_low0"]:
                    probs_low(b, 0)
                if ph == DVE_AT["PT_low1"]:
                    probs_low(b, 1)
                if ph == DVE_AT["elu_neg0"]:
                    elu_negative(b, 0)
                if ph == DVE_AT["prob1"]:
                    softmax_probs(b, 1)
                if ph == DVE_AT["PT_low2"]:
                    probs_low(b, 2)
                if ph == DVE_AT["elu_sum0"]:
                    elu_sum(b, 0)
                if ph == DVE_AT["PT_low3"]:
                    probs_low(b, 3)
                if ph == DVE_AT["elu_neg1"]:
                    elu_negative(b, 1)
                if ph == DVE_AT["elu_sum1"]:
                    elu_sum(b, 1)
                if ph == DVE_AT["X2_low0"]:
                    features2_low(b, 0)
                if ph == DVE_AT["X2_low1"]:
                    features2_low(b, 1)
                if ph == DVE_AT["source2"]:
                    source2(b)
                if ph == DVE_AT["max2"]:
                    softmax_max(b, 2)
                if ph == DVE_AT["prob2"]:
                    softmax_probs(b, 2)
                if ph == DVE_AT["PT_low4"]:
                    probs_low(b, H)
                if ph == DVE_AT["x1"]:
                    residual1(b, p, par, base)
                if ph == DVE_AT["norm2"]:
                    wait_alone(dve, (s_x1, b + 1))
                    layer_norm(b, 1, [yacc[:, tokens(p, par, j), :] for j in range(NJ)], s_ln2)
                if ph == DVE_AT["T2_low"]:
                    ffn_x_low(b, p, par)
                if ph == DVE_AT["top"]:
                    router_top(b)
                if ph == DVE_AT["comb"]:
                    router_weights(b, p, par)
                if ph == DVE_AT["norm1_next"] and ahead:
                    norm1(b + 1)

            def pair_weights(i, base, p, par):
                dve.wait_ge(s_comb, base + SB_B)
                dve.wait_ge(s_y, START + GROUPS * i)
                nc.vector.tensor_copy(cw[:, :, :], comb[:, par * SB_B * NJ:(par + 1) * SB_B * NJ,
                                                        bass.ds(p * EI, EI)]).then_inc(s_cw, 1)
                dve.wait_ge(s_cw, i + 1)
                dve.wait_ge(s_x1, base + SB_B)

            def gate_product(i, u):
                dve.wait_ge(s_th, UNITS * i + u + 1)
                hu = hb[:, u % 2, :]
                nc.vector.scalar_tensor_tensor(hu, hu, 1.0, pG[u % 2][:, :], ALU.add, ALU.mult).then_inc(s_a, 1)

            def hidden(i, u):
                dve.wait_ge(s_u, UNITS * i + u + 1)
                dve.wait_ge(s_a, UNITS * i + u + 1 + CREDIT)
                hu = hb[:, u % 2, :]
                nc.vector.tensor_tensor(hu, hu, pU[u % 2][:, :], ALU.mult).then_inc(s_h, 1)

            def add_y(i, g, half):
                el, blk = divmod(g, NBLK)
                dve.wait_ge(s_dn, UNITS * i + (g + 1) * FT + CREDIT)
                dve.wait_ge(s_y, START + GROUPS * i + g)
                for tt in range(TT):
                    tile = blk * TT + tt
                    acc = yacc[:, bass.ds(half * (SB_B * NJ) + tile, 1), :]
                    last = nc.vector.scalar_tensor_tensor(acc, pY[tt // 2][:, tt % 2, :], cw[:, tile, el:el + 1], acc,
                                                          ALU.mult, ALU.add)
                last.then_inc(s_y, 1)

            def graph_only(b, p, par):
                links[0] = 0
                for ph in range(PHASES):
                    graph_phase(b, p, par, None, ph)
                assert links[0] == DVE_LINKS, links[0]

            def ffn(base, p, par, graph=True, ahead=True, first=False, last=False):
                i = base + p
                links[0] = 0
                for u in range(UNITS):
                    gate_product(i, u)
                    if graph:
                        graph_phase(i + SB_B, p, 1 - par, base, 3 * u, ahead)
                        graph_phase(i + SB_B, p, 1 - par, base, 3 * u + 1, ahead)
                    hidden(i, u)
                    if graph:
                        graph_phase(i + SB_B, p, 1 - par, base, 3 * u + 2, ahead)
                    if u == LAG - 1:
                        if not first:
                            add_y(i - 1, GROUPS - 1, (i - 1) // SB_B % 2)
                        pair_weights(i, base, p, par)
                    elif u % FT == LAG - 1:
                        add_y(i, u // FT - 1, par)
                if last:
                    add_y(i, GROUPS - 1, par)

            norm1(0)
            run_iterations(dve, graph_only, ffn)

        @block.tensor
        def _(pe):
            def pairs(a, b):
                return ((a[0], b[0]), (a[1], b[0]), (a[0], b[1]))

            def product(dst, terms):
                for n, (lhsT, rhs) in enumerate(terms):
                    last = nc.tensor.matmul(dst, lhsT, rhs, start=(n == 0), stop=(n == len(terms) - 1))
                return last

            def transpose_norm(b, bank, done):
                for k in range(KD):
                    for j in range(NJ):
                        last = nc.tensor.transpose(bank[:, k * N + j * P:k * N + (j + 1) * P], xn[:, j, k * P:(k + 1) * P],
                                                   ident[:, :])
                last.then_inc(done, 1)

            def T1(b):
                pe.wait_ge(s_ln1, b + 1)
                pe.wait_ge(s_lr, START + b)
                transpose_norm(b, pA, s_T1)

            def MT(b):
                pe.wait_ge(s_mask, b + 1)
                pe.wait_ge(s_lg, START + b)
                for jt in range(NJ):
                    for js in range(NJ):
                        last = nc.tensor.transpose(maskT[:, jt * N + js * P:jt * N + (js + 1) * P],
                                                   mask[:, js, jt * P:(jt + 1) * P], ident_b[:, :])
                last.then_inc(s_MT, 1)

            def RW(b):
                pe.wait_ge(s_nT, b + 1)
                product(pA[:, 0:N], [(v[:, k, :], n[:, k, :]) for k in range(KD) for v, n in pairs(v1s, nTs)]).then_inc(s_RW, 1)

            def X1(b, j):
                if j == 0:
                    pe.wait_ge(s_mb, b + 1)
                else:
                    pe.wait_ge(s_xll, 2 * b + 1)
                product(pB[:, :], [(n[:, k, j * P:(j + 1) * P], w[:, k, :]) for k in range(KD)
                                   for n, w in pairs(nTs, W1s)]).then_inc(s_X1, 1)

            def CT(b):
                wait_alone(pe, (s_rwl, b + 1))
                for j in range(NJ):
                    last = nc.tensor.transpose(pA[:, j * 2 * H:(j + 1) * 2 * H], rows_f[:, j * P:(j + 1) * P],
                                               ident[0:2 * H, 0:2 * H])
                last.then_inc(s_CT, 1)

            def SB(b, g):
                if g == 0:
                    pe.wait_ge(s_cols, b + 1)
                else:
                    pe.wait_ge(s_xll, 2 * b + 2)
                for h in range(2):
                    last = product((pA, pB)[g][:, h * N:(h + 1) * N],
                                   [(head_row[:, 2 * g + h, :], r[:, :]) for r in rows_s])
                last.then_inc(s_SB, 1)

            def PT(b, h):
                if h in (0, 1):
                    pe.wait_ge(s_pn, 3 * b + 1)
                    pe.wait_ge(s_max, START + 3 * b + h + 1)
                elif h in (2, 3):
                    pe.wait_ge(s_pn, 3 * b + 2)
                    if h == 2:
                        pe.wait_ge(s_PTl, 5 * b + 2)
                    else:
                        pe.wait_ge(s_z, 2 * b + 1)
                else:
                    pe.wait_ge(s_pn, 3 * b + 3)
                    pe.wait_ge(s_x2l, 2 * b + 2)
                for js in range(NJ):
                    for jt in range(NJ):
                        last = nc.tensor.transpose(bank_PT[h][:, js * N + jt * P:js * N + (jt + 1) * P],
                                                   e1[:, h % H, jt, js * P:(js + 1) * P], ident[:, :])
                last.then_inc(s_PT, 1)

            def A1(b, h):
                pe.wait_ge(s_PTl, 5 * b + h + 1)
                if h == 2:
                    pe.wait_ge(s_PTl, 5 * b + 3)
                product(bank_A1[h // 2][:, (h % 2) * N:(h % 2 + 1) * N],
                        [(xl[:, j, h * P:(h + 1) * P], pt[:, h % 2, j, :]) for j in range(NJ)
                         for xl, pt in pairs(xls, PTs)]).then_inc(s_A1, 1)

            def X2(b, j):
                pe.wait_ge(s_h1, START + 2 * b + 2)
                product(bank_X2[j][:, 0:W2N], [(h[:, k, j * P:(j + 1) * P], w[:, k, :]) for k in range(KF)
                                               for h, w in pairs(h1s, W2s)]).then_inc(s_X2, 1)

            def B2(b):
                pe.wait_ge(s_a2, b + 1)
                for j in range(NJ):
                    last = product(pA[:, j * P:(j + 1) * P], [(a[:, j, :], ident_r[:, :]) for a in a2s])
                last.then_inc(s_B2, 1)

            def A2(b):
                pe.wait_ge(s_PTl, 5 * b + 5)
                pe.wait_ge(s_max, START + 3 * b + 3)
                for jt in range(NJ):
                    last = product(pA[:, jt * D:(jt + 1) * D], [(pt[:, 0, js, jt * P:(jt + 1) * P], xl[:, js, :])
                                                                for js in range(NJ) for pt, xl in pairs(PTs, nTs)])
                last.then_inc(s_A2, 1)

            def T2(b):
                pe.wait_ge(s_ln2, b + 1)
                transpose_norm(b, pB, s_T2)

            def RT(b, p, par):
                pe.wait_ge(s_fT, b + 1)
                at = bass.ds(p * N + par * SB_T, N)
                product(pA[:, 0:N], [(r[:, k, :], xt[:, k, at]) for k in range(KD) for r, xt in pairs(rws, xTs)]).then_inc(s_RT, 1)

            def LC(b):
                wait_alone(pe, (s_lr, START + b + 1))
                for j in range(NJ):
                    last = nc.tensor.transpose(pB[:, j * E:(j + 1) * E], lrows[:, j * P:(j + 1) * P], ident[0:E, 0:E])
                last.then_inc(s_LC, 1)

            def graph_phase(b, p, par, ph):
                if ph == PE_AT["T1"]:
                    T1(b)
                if ph == PE_AT["MT"]:
                    MT(b)
                if ph == PE_AT["RW"]:
                    RW(b)
                if ph == PE_AT["X1_0"]:
                    X1(b, 0)
                if ph == PE_AT["CT"]:
                    CT(b)
                if ph == PE_AT["X1_1"]:
                    X1(b, 1)
                if ph == PE_AT["SB0"]:
                    SB(b, 0)
                if ph == PE_AT["SB1"]:
                    SB(b, 1)
                if ph == PE_AT["PT0"]:
                    PT(b, 0)
                if ph == PE_AT["PT1"]:
                    PT(b, 1)
                if ph == PE_AT["A1_0"]:
                    A1(b, 0)
                if ph == PE_AT["A1_1"]:
                    A1(b, 1)
                if ph == PE_AT["PT2"]:
                    PT(b, 2)
                if ph == PE_AT["PT3"]:
                    PT(b, 3)
                if ph == PE_AT["A1_2"]:
                    A1(b, 2)
                if ph == PE_AT["A1_3"]:
                    A1(b, 3)
                if ph == PE_AT["X2_0"]:
                    X2(b, 0)
                if ph == PE_AT["X2_1"]:
                    X2(b, 1)
                if ph == PE_AT["B2"]:
                    B2(b)
                if ph == PE_AT["PT4"]:
                    PT(b, H)
                if ph == PE_AT["A2"]:
                    A2(b)
                if ph == PE_AT["T2"]:
                    T2(b)
                if ph == PE_AT["RT"]:
                    RT(b, p, par)
                if ph == PE_AT["LC"]:
                    LC(b)

            def gate(i, u, par):
                if u % (NBLK * FT) == 0:
                    pe.wait_ge(s_wl, NWI * i + NW * (u // (NBLK * FT)) + 1)
                pe.wait_ge(s_a, UNITS * i + u + 1)
                expand(we1, pG, u, par).then_inc(s_g, 1)

            def up(i, u, par):
                if u % (NBLK * FT) == 0:
                    pe.wait_ge(s_wl, NWI * i + NW * (u // (NBLK * FT)) + 2)
                pe.wait_ge(s_h, UNITS * i + u + 1)
                expand(we3, pU, u, par).then_inc(s_u, 1)

            def expand(we, bank, u, par):
                el, blk, ft = u // (NBLK * FT), u // FT % NBLK, u % FT
                at = slice(par * SB_T + blk * BLK, par * SB_T + (blk + 1) * BLK)
                return product(bank[u % 2][:, :], [(w[:, k, ft * P:(ft + 1) * P], xt[:, k, at]) for k in range(KD)
                                                   for w, xt in pairs(we[el], xTs)])

            def down(i, u):
                el, ft = u // (NBLK * FT), u % FT
                if u % (NBLK * FT) == 0:
                    pe.wait_ge(s_wl, NWI * i + NW * el + NW)
                if ft == 0:
                    pe.wait_ge(s_y, START + GROUPS * i + u // FT)
                pe.wait_ge(s_hl, UNITS * i + u + 1 + CREDIT)
                for tt in range(TT):
                    ts = slice(tt * P, (tt + 1) * P)
                    for n, (h, w) in enumerate(pairs(hhs, we2[el])):
                        last = nc.tensor.matmul(pY[tt // 2][:, tt % 2, :], h[:, u % 2, ts], w[:, ft, :],
                                                start=(ft == 0 and n == 0 and tt % 2 == 0),
                                                stop=(ft == FT - 1 and n == 2), skip_group_check=True)
                last.then_inc(s_dn, 1)

            def graph_only(b, p, par):
                for ph in range(PHASES):
                    graph_phase(b, p, par, ph)

            def ffn(base, p, par, graph=True, ahead=True, first=False, last=False):
                i = base + p
                pe.wait_ge(s_fT, base + SB_B)
                for u in range(UNITS):
                    gate(i, u, par)
                    if graph:
                        graph_phase(i + SB_B, p, 1 - par, 3 * u)
                    up(i, u, par)
                    if graph:
                        graph_phase(i + SB_B, p, 1 - par, 3 * u + 1)
                    if u >= LAG:
                        down(i, u - LAG)
                    elif not first:
                        down(i - 1, UNITS + u - LAG)
                    if graph:
                        graph_phase(i + SB_B, p, 1 - par, 3 * u + 2)
                if last:
                    for u in range(UNITS - LAG, UNITS):
                        down(i, u)

            pe.sem_inc(s_dn, CREDIT)
            for s_ in (s_MT, s_SB, s_A1, s_A2, s_PT, s_X2):
                pe.sem_inc(s_, START)
            pe.wait_ge(s_prepd, 1)
            pe.wait_ge(s_cr, 1)
            run_iterations(pe, graph_only, ffn)


_INS = ['x', 'adj', 'L0_gnn_W1', 'L0_gnn_att_src1', 'L0_gnn_att_dst1', 'L0_gnn_b1', 'L0_gnn_W2', 'L0_gnn_att_src2',
        'L0_gnn_att_dst2', 'L0_gnn_b2', 'L0_ffn_router_w', 'L0_ffn_w1', 'L0_ffn_w2', 'L0_ffn_w3']
_OUTS = [((32, 256, 256), 'float32')]


def kernel(**inputs):
    import numpy as _np
    import concourse.bacc as _bacc
    from concourse import mybir as _mybir
    from concourse.bass_utils import run_bass_kernel_spmd as _run

    nc = _bacc.Bacc("TRN2", target_bir_lowering=False, num_devices=1)
    arrays, args = {}, []
    for name in _INS:
        a = _np.ascontiguousarray(inputs[name])
        arrays[f"in_{name}_dram"] = a
        args.append(nc.dram_tensor(f"in_{name}_dram", a.shape, _mybir.dt.from_np(a.dtype), kind="ExternalInput").ap())
    for i, (shape, dtype) in enumerate(_OUTS):
        dt = _mybir.dt.from_np(_np.dtype(dtype))
        args.append(nc.dram_tensor(f"out_{i}_dram", shape, dt, kind="ExternalOutput").ap())
    gat_moe_kernel(nc, *args)
    r = _run(nc, [arrays], core_ids=[0])
    got = tuple(r.results[0][f"out_{i}_dram"] for i in range(len(_OUTS)))
    return got[0]
```

```python
from contextlib import ExitStack

import concourse.bass as bass
from concourse import mybir

ALU = mybir.AluOpType
ACT = mybir.ActivationFunctionType
F32 = mybir.dt.float32
F32R = mybir.dt.float32r
BF16 = mybir.dt.bfloat16
I32 = mybir.dt.int32
U32 = mybir.dt.uint32
AX_X = mybir.AxisListType.X

P = 128
NEG_SLOPE = 0.2
LN_EPS = 1e-5
MASKED = 1e30
LOWEST = -3.0e38
RSQRT_SEED = float(0x5f3759df - (1 << 22) - (1 << 31))
NEWTON_STEPS = 3


def gat_moe_kernel(nc, x, adj, W1, a_src1, a_dst1, b1, W2, a_src2, a_dst2, b2, router_w, w1, w2, w3, out):
    B, N, D = x.shape
    H, FH = a_src1.shape
    HF = H * FH
    E, _, F = w1.shape
    NJ = N // P
    KD = D // P
    KF = HF // P
    FT = F // P
    BLK = 512
    SB_B = 4
    SB_T = SB_B * N
    NBLK = SB_T // BLK
    TT = BLK // P
    NSB = B // SB_B
    EI = E // SB_B
    UNITS = EI * NBLK * FT
    WC = KD * F
    W2N = D + 2
    assert N == 256 and D == 256 and FH == P and WC == FT * D == 1024 and NSB % 2 == 0

    with ExitStack() as ctx:
        def sb(name, shape, dt):
            return ctx.enter_context(nc.sbuf_tensor(name, shape, dt))

        def sem(name):
            return ctx.enter_context(nc.semaphore(name))

        ident = sb("ident", [P, P], F32)
        ident_r = sb("ident_r", [P, P], F32R)
        ident_b = sb("ident_b", [P, P], BF16)
        eye = sb("eye", [P, NJ, N], BF16)
        head_row = sb("head_row", [2 * H, H, P], F32R)
        expert_id = sb("expert_id", [P, E], F32)
        W1s = [sb(f"W1_{s}", [P, KD, HF], F32R) for s in "hl"]
        W2s = [sb(f"W2_{s}", [P, KF, W2N], F32R) for s in "hl"]
        v1s = [sb(f"v1_{s}", [P, KD, P], F32R) for s in "hl"]
        rws = [sb(f"rw_{s}", [P, KD, P], F32R) for s in "hl"]
        v2f = sb("v2f", [P, KF, 2], F32)
        b1T = sb("b1T", [P, H], F32)
        b2b = sb("b2b", [P, D], F32)

        stage = sb("stage", [P, 2, WC], F32)
        we1 = [[sb(f"we1_{e}{s}", [P, KD, F], F32R) for s in "hl"] for e in range(EI)]
        we3 = [[sb(f"we3_{e}{s}", [P, KD, F], F32R) for s in "hl"] for e in range(EI)]
        we2 = [[sb(f"we2_{e}{s}", [P, FT, D], F32R) for s in "hl"] for e in range(EI)]

        xTs = [sb(f"xT_{s}", [P, KD, 2 * SB_T], F32R) for s in "hl"]
        yacc = sb("yacc", [P, 2 * SB_B * NJ, D], F32)
        comb = sb("comb", [P, 2 * SB_B * NJ, E], F32)
        cw = sb("cw", [P, SB_B * NJ, EI], F32)
        hb = sb("hb", [P, 2, BLK], F32)
        hhs = [sb(f"hh_{s}", [P, 2, BLK], F32R) for s in "hl"]

        xb = sb("xb", [P, NJ, D], F32)
        adjb = sb("adjb", [P, NJ, N], I32)
        xn1 = sb("xn1", [P, NJ, D], F32)
        xn2 = sb("xn2", [P, NJ, D], F32)
        mask = sb("mask", [P, NJ, N], BF16)
        mbias = sb("mbias", [P, NJ, N], F32)
        nTs = [sb(f"nT_{s}", [P, KD, N], F32R) for s in "hl"]
        rows_f = sb("rows_f", [2 * H, N], F32)
        rows_s = [sb(f"rows_{s}", [2 * H, N], F32R) for s in "hl"]
        lrows = sb("lrows", [E, N], F32)
        cols = sb("cols", [P, NJ, 2 * H], F32)
        xls = [sb(f"xl_{s}", [P, NJ, HF], F32R) for s in "hl"]
        sc = sb("sc", [P, 2, NJ, N], F32)
        e1 = sb("e1", [P, H, NJ, N], F32)
        e2 = sb("e2", [P, 2, NJ, N], F32)
        PTs = [sb(f"PT_{s}", [P, 2, NJ, N], F32R) for s in "hl"]
        z = sb("z", [P, H, N], F32)
        h1s = [sb(f"h1_{s}", [P, KF, N], F32R) for s in "hl"]
        a2c = sb("a2c", [P, NJ, 2], F32)
        a2s = [sb(f"a2_{s}", [P, NJ, P], F32R) for s in "hl"]
        st = sb("st", [P, NJ, 6], F32)
        mv = sb("mv", [P, NJ, 2], F32)
        nw = sb("nw", [P, 4, NJ], F32)
        mx = sb("mx", [P, NJ, 2], F32)
        mm_ = sb("mm_", [P, NJ, 2], F32)
        bi1 = sb("bi1", [P, NJ, H], F32)
        bi2 = sb("bi2", [P, NJ, H], F32)
        sm = sb("sm", [P, NJ, 2], F32)
        rs = sb("rs", [P, NJ, 2], F32)
        lg = sb("lg", [P, NJ, E], F32)
        top = sb("top", [P, NJ, 8], F32)
        topi = sb("topi", [P, NJ, 8], U32)
        topf = sb("topf", [P, NJ, 8], F32)
        gap = sb("gap", [P, NJ], F32)
        eg = sb("eg", [P, NJ], F32)
        wts = sb("wts", [P, 3, NJ], F32)
        oh = sb("oh", [P, 2, NJ, E], F32)

        pG = [ctx.enter_context(nc.psum_tensor(f"pG{i}", [P, BLK], F32)) for i in range(2)]
        pU = [ctx.enter_context(nc.psum_tensor(f"pU{i}", [P, BLK], F32)) for i in range(2)]
        pY = [ctx.enter_context(nc.psum_tensor(f"pY{i}", [P, 2, D], F32)) for i in range(2)]
        pA = ctx.enter_context(nc.psum_tensor("pA", [P, 512], F32))
        pB = ctx.enter_context(nc.psum_tensor("pB", [P, 512], F32))

        maskT = pB[:, 0:NJ * N // 2].bitcast(BF16)
        bank_PT = [pA, pB, pB, pA, pB]
        bank_A1 = [pA, pB]
        bank_X1 = [pA, pB]
        bank_X2 = [pA, pB]

        def flat(t_):
            return t_[:, :, :].rearrange("p a b -> p (a b)")

        def fold(t_, n=2):
            return t_[:, :].rearrange("p (a b) -> p a b", a=n)

        def scores(g):
            return z[:, :, :].rearrange("p (a j) n -> p a j n", a=2) if g == 1 else sc

        def slot(g, h):
            return 2 * (g % 2) + h

        def w2_products(n):
            return e1[:, 2 * n:2 * n + 2, :, :].rearrange("p a j n -> p (a j) n")

        s_cin = sem("biases_and_router_loaded")
        s_av = sem("attention_vectors_loaded")
        s_gwh = sem("gat_weights_high")
        s_gwl = sem("gat_weights_low")
        s_v2p = sem("attention2_products")
        s_w12 = sem("gat_weights_loaded")
        s_cz = sem("const_zeroed")
        s_cid = sem("const_built")
        s_cr = sem("const_rounded")
        s_prep = sem("prep_order")
        s_prepd = sem("prep_done")
        s_x = sem("x_loaded")
        s_adj = sem("adj_loaded")
        s_xb2 = sem("bias2_added")
        s_maskp = sem("mask_marks_2_per_graph")
        s_mask = sem("mask_ready")
        s_dg = sem("dve_graph_order")
        s_norm = sem("dve_norm_order")
        s_dr = sem("dve_router_order")
        s_ln1 = sem("ln1_ready")
        s_T1 = sem("T1_done")
        s_nTh = sem("nT_high")
        s_nT = sem("nT_ready")
        s_MT = sem("mask_transposed")
        s_mb = sem("mask_bias_ready")
        s_RW = sem("score_rows_done")
        s_rwc = sem("score_rows_copied")
        s_rwl = sem("score_rows_low")
        s_CT = sem("score_cols_done")
        s_cols = sem("score_cols_copied")
        s_X1 = sem("features1_done_2_per_graph")
        s_xlh = sem("features1_high_2_per_graph")
        s_xll = sem("features1_low_2_per_graph")
        s_SB = sem("source_scores_spread_2_per_graph")
        s_max = sem("score_bias_ready_3_per_graph")
        s_exp = sem("exps_done_5_per_graph")
        s_larger = sem("larger_exps_taken_5_per_graph")
        s_pn = sem("probs_ready_5_per_graph")
        s_PT = sem("probs_transposed_5_per_graph")
        s_PTh = sem("probsT_high_5_per_graph")
        s_PTl = sem("probsT_low_5_per_graph")
        s_A1 = sem("attended1_done_4_per_graph")
        s_z = sem("attended1_biased_2_per_graph")
        s_zn = sem("elu_negative_part_2_per_graph")
        s_ze = sem("elu_exp_2_per_graph")
        s_zf = sem("elu_done_2_per_graph")
        s_h1h = sem("h1_high_2_per_graph")
        s_h1 = sem("h1_ready_2_per_graph")
        s_X2 = sem("features2_done_2_per_graph")
        s_x2h = sem("features2_high_2_per_graph")
        s_x2l = sem("features2_low_2_per_graph")
        s_a2 = sem("source2_columns_ready")
        s_B2 = sem("source2_scores_spread")
        s_A2 = sem("attended2_done")
        s_x1 = sem("gnn_residual_ready")
        s_ln2 = sem("ln2_ready")
        s_T2 = sem("T2_done")
        s_fTh = sem("ffn_xT_high")
        s_fT = sem("ffn_xT_ready")
        s_RT = sem("router_rows_done")
        s_lr = sem("router_rows_copied")
        s_LC = sem("router_cols_done")
        s_lg = sem("router_cols_copied")
        s_gap = sem("logit_gap_ready")
        s_eg = sem("gap_exp_done")
        s_comb = sem("combine_ready")
        s_wst = [sem("chunk_loaded_0"), sem("chunk_loaded_1")]
        s_wh = sem("chunk_high")
        s_wl = sem("chunk_split")
        s_g = sem("gate_done")
        s_u = sem("up_done")
        s_th = sem("tanh_done")
        s_a = sem("gate_used")
        s_h = sem("hidden_ready")
        s_hh = sem("hidden_high")
        s_hl = sem("hidden_low")
        s_dn = sem("down_done")
        s_cw = sem("weights_of_pair_ready")
        s_y = sem("y_added")
        s_out = sem("out_stored")

        CREDIT = 2
        START = 1
        LAG = 2
        GROUPS = EI * NBLK
        NORM_LINKS = 5 + 2 * NEWTON_STEPS
        DVE_LINKS = 14
        ROUTER_LINKS = 7
        HEADS = H + 1
        NW = 3
        NWI = NW * EI

        block = ctx.enter_context(nc.Block())

        def run_iterations(eng, graph_only, ffn):
            graph_only(0, 0, 0, router=False)
            with eng.Fori(1, SB_B) as p:
                graph_only(p, p, 0)
            ffn(0, 0, 0, first=True)
            with eng.Fori(0, NSB // 2 - 1) as s2:
                with eng.Fori(1, SB_B) as p:
                    ffn(s2 * (2 * SB_B), p, 0)
                with eng.Fori(0, SB_B) as p:
                    ffn(s2 * (2 * SB_B) + SB_B, p, 1)
                ffn(s2 * (2 * SB_B) + 2 * SB_B, 0, 0)
            with eng.Fori(1, SB_B - 1) as p:
                ffn(B - 2 * SB_B, p, 0)
            ffn(B - 2 * SB_B, SB_B - 1, 0, ahead=False)
            ffn(B - SB_B, 0, 1, graph=False)
            with eng.Fori(1, SB_B - 1) as p:
                ffn(B - SB_B, p, 1, graph=False, router=False)
            ffn(B - SB_B, SB_B - 1, 1, graph=False, router=False, last=True)

        def wait_alone(eng, *waits):
            counts = [(s, v if isinstance(v, int) else eng.to_reg(v)) for s, v in waits]
            eng.wait_ge(s_cz, 1)
            for s, v in counts:
                eng.wait_ge(s, v)

        @block.sync
        def _(sp):
            def load_graph(b, first=False):
                if not first:
                    sp.wait_ge(s_x1, b)
                sp.dma_start(xb[:, :, :], x[bass.ds(b, 1)].rearrange("o (j p) d -> p (o j) d", p=P)).then_inc(s_x, 16)
                if not first:
                    sp.wait_ge(s_maskp, 2 * b)
                sp.dma_start(adjb[:, :, :], adj[bass.ds(b, 1)].rearrange("o (j p) d -> p (o j) d", p=P)).then_inc(s_adj, 16)

            def load_chunk(e, c, n, first=False):
                slot = (e * NW + c) % 2
                if not first:
                    sp.wait_ge(s_wl, n - 1)
                else:
                    sp.wait_ge(s_prepd, 1)
                dst = stage[:, slot, :].rearrange("p (k n) -> p k n", k=KD if c < 2 else FT)
                src = (w1, w3, w2)[c][e].rearrange("(k p) n -> p k n", p=P)
                sp.dma_start(dst, src).then_inc(s_wst[slot], 16)

            def load_expert(e, n0, first=False):
                for c in range(NW):
                    load_chunk(e, c, n0 + c, first and c < 2)

            sp.sem_inc(s_out, START)
            load_graph(0, True)
            for n, (w, k) in enumerate(((W1, KD), (W2, KF))):
                sp.dma_start(stage[:, n, :].rearrange("p (k n) -> p k n", k=k),
                             w.rearrange("(k p) n -> p k n", p=P)).then_inc(s_w12, 16)
            for n, a in enumerate((a_src1, a_dst1)):
                sp.dma_start(hb[:, n, :], a.rearrange("(o h) f -> o (h f)", o=1).broadcast_to([P, HF])).then_inc(s_av, 16)
            for n, a in enumerate((a_src2, a_dst2)):
                sp.dma_start(e2[:, 0, n, :], a.broadcast_to([P, D])).then_inc(s_av, 16)
            sp.dma_start(b2b[:, :], b2.rearrange("(o d) -> o d", o=1).broadcast_to([P, D])).then_inc(s_cin, 16)
            sp.wait_ge(s_cz, 1)
            sp.dma_start(z[:, 0:KD, P:P + E], router_w.rearrange("(k p) e -> p k e", p=P)).then_inc(s_cin, 16)
            sp.dma_start(b1T[:, :], b1.rearrange("(h f) -> f h", f=P), allow_slow_non_contiguous=True).then_inc(s_cin, 16)
            load_expert(0, 0, True)
            with sp.Fori(1, SB_B + 1) as b:
                load_graph(b)

            def store(s, par):
                for blk in range(NBLK):
                    sp.wait_ge(s_y, START + NBLK * E * (s + 1) - (NBLK - 1 - blk))
                    g0, gs = BLK // N * blk, BLK // N
                    t0 = par * SB_B * NJ + TT * blk
                    sp.dma_start(out[bass.ds(s * SB_B + g0, gs)].rearrange("g (j p) d -> p (g j) d", p=P),
                                 yacc[:, t0:t0 + TT, :]).then_inc(s_out, 16)

            def iteration(s, q, last_sb=False, ahead=True):
                if q > 0:
                    load_expert(EI * q + 1, s * NW * E + NW * (EI * q + 1))
                if not (last_sb and q == SB_B - 1):
                    load_expert((EI * q + EI) % E, s * NW * E + NW * (EI * q + EI))
                if ahead:
                    load_graph(s * SB_B + q + SB_B + 1)

            load_expert(1, NW)
            with sp.Fori(0, NSB // 2 - 1) as sh:
                for par in range(2):
                    s = sh * 2 + par
                    for q in range(SB_B):
                        iteration(s, q)
                    load_expert(1, (s + 1) * NW * E + NW)
                    store(s, par)
            for q in range(SB_B):
                iteration(NSB - 2, q, ahead=q < SB_B - 1)
            load_expert(1, (NSB - 1) * NW * E + NW)
            store(NSB - 2, 0)
            for q in range(SB_B):
                iteration(NSB - 1, q, last_sb=True, ahead=False)
            store(NSB - 1, 1)
            sp.wait_ge(s_out, START + 16 * NBLK * NSB)

        PHASES = 3 * UNITS
        PE_AT = dict(T1=1, MT=4, RW=3, X1_0=9, CT=5, X1_1=11, SB0=6, SB1=6, PT0=14, PT1=15, A1_0=17, A1_1=20, PT2=22,
                     PT3=22, A1_2=24, A1_3=24, X2_head=28, X2_0=29, X2_1=30, B2=32, PT4=36, A2=38, T2=46, RT=0, LC=1)
        ACT_AT = dict(T1_high=0, mask_bias=4, rows=3, X1_high0=9, X1_high1=11, exp0=7, PT_high0=13, PT_high1=15,
                      exp1=16, bias0=19, elu_exp0=19, PT_high2=21, PT_high3=21, bias1=25, elu_exp1=25, h1_high0=23,
                      h1_high1=25, X2_high0=29, X2_high1=31, exp2=34, PT_high4=35, T2_high=46, RT_rows=0, gap_exp=4)
        DVE_AT = dict(T1_low=1, rows_low=3, X1_low0=9, cols=5, X1_low1=12, max0=6, prob0=11, max1=7, PT_low0=15,
                      PT_low1=15, elu_neg0=20, prob1=19, PT_low2=20, elu_sum0=22, PT_low3=21, elu_neg1=24,
                      elu_sum1=25, X2_low0=29, X2_low1=30, source2=31, max2=32, prob2=35, PT_low4=35, x1=38, norm2=38,
                      root2=44, T2_low=47, top=1, comb=5, norm1_next=46, root1_next=47)
        POOL_AT = dict(mask=0, bias2=3, h1_low0=23, h1_low1=23)
        CHUNKS_FIRST = (20, 23, 26)
        PE_FIRST = dict(T1=2, MT=2, RW=4, X1_0=9, CT=6, X1_1=11, SB0=8, SB1=9, PT0=11, PT1=12, A1_0=14, A1_1=14,
                        PT2=16, PT3=17, A1_2=18, A1_3=18, X2_head=22, X2_0=22, X2_1=23, B2=23, PT4=25, A2=26, T2=28,
                        RT=0, LC=0)
        ACT_FIRST = dict(T1_high=2, mask_bias=2, rows=4, X1_high0=8, X1_high1=10, exp0=9, PT_high0=11, PT_high1=12,
                         exp1=11, bias0=15, elu_exp0=15, PT_high2=16, PT_high3=17, bias1=20, elu_exp1=20, h1_high0=16,
                         h1_high1=20, X2_high0=21, X2_high1=22, exp2=23, PT_high4=25, T2_high=28, RT_rows=0, gap_exp=5)
        DVE_FIRST = dict(T1_low=3, rows_low=4, X1_low0=9, cols=6, X1_low1=11, max0=8, prob0=10, max1=9, PT_low0=10,
                         PT_low1=12, elu_neg0=15, prob1=14, PT_low2=16, elu_sum0=15, PT_low3=17, elu_neg1=18,
                         elu_sum1=18, X2_low0=22, X2_low1=22, source2=22, max2=23, prob2=24, PT_low4=25, x1=27,
                         norm2=27, root2=27, T2_low=29, top=1, comb=7, norm1_next=29, root1_next=30)
        POOL_FIRST = dict(mask=1, bias2=3, h1_low0=15, h1_low1=20)

        @block.gpsimd
        def _(pool):
            nc.gpsimd.memset(ident[:, :], 0.0)
            nc.gpsimd.memset(eye[:, :, :], 0.0)
            nc.gpsimd.memset(z[:, :, :], 0.0).then_inc(s_cz, 1)
            for e in range(E):
                nc.gpsimd.memset(expert_id[:, e:e + 1], float(e))
            pool.wait_ge(s_cz, 1)
            nc.gpsimd.affine_select(out=ident[:, :], in_=ident[:, :], compare_op=ALU.not_equal, fill=1.0, base=0,
                                    pattern=[[-1, P]], channel_multiplier=1)
            nc.gpsimd.affine_select(out=eye[:, :, :], in_=eye[:, :, :], compare_op=ALU.not_equal, fill=1.0, base=0,
                                    pattern=[[P, NJ], [-1, N]], channel_multiplier=1)
            spread = z[0:2 * H, 0:H, 0:P]
            nc.gpsimd.affine_select(out=spread, in_=spread, compare_op=ALU.not_equal, fill=1.0, base=0,
                                    pattern=[[-1, H], [0, P]], channel_multiplier=1).then_inc(s_cid, 1)
            pool.wait_ge(s_cid, 1)
            nc.gpsimd.tensor_copy(ident_r[:, :], ident[:, :])
            nc.gpsimd.tensor_copy(ident_b[:, :], ident[:, :])
            nc.gpsimd.tensor_copy(head_row[:, :, :], spread).then_inc(s_cr, 1)
            pool.sem_inc(s_hl, CREDIT)
            pool.sem_inc(s_h1, START)

            def chunk_low(el, c, i, ahead):
                k = NW * el + c
                dh, dl = (flat((we1, we3, we2)[c][el][s]) for s in range(2))
                pool.wait_ge(s_wh, NWI * (i + ahead) + k + 1)
                nc.gpsimd.tensor_tensor(dl, stage[:, k % 2, :], dh, ALU.subtract).then_inc(s_wl, 1)

            def graph_inputs(b):
                wait_alone(pool, (s_adj, 16 * b + 16), (s_MT, START + b))
                nc.gpsimd.tensor_scalar(mask[:, :, :], adjb[:, :, :], 0.0, None, ALU.is_gt).then_inc(s_maskp, 1)
                pool.wait_ge(s_maskp, 2 * b + 1)
                nc.gpsimd.tensor_tensor(mask[:, :, :], mask[:, :, :], eye[:, :, :], ALU.add).then_inc(s_maskp, 1)
                wait_alone(pool, (s_maskp, 2 * b + 2))
                nc.gpsimd.tensor_scalar(mask[:, :, :], mask[:, :, :], 1.0, None, ALU.min).then_inc(s_mask, 1)

            def graph_bias(b):
                pool.wait_ge(s_ln1, b + 1)
                nc.gpsimd.tensor_tensor(xb[:, :, :], xb[:, :, :], b2b[:, :].unsqueeze(1).broadcast_to([P, NJ, D]),
                                        ALU.add).then_inc(s_xb2, 1)

            def graph_h1_low(b, g):
                pool.wait_ge(s_h1h, 2 * b + g + 1)
                hs = slice(2 * g, 2 * g + 2)
                nc.gpsimd.tensor_tensor(h1s[1][:, hs, :], z[:, hs, :], h1s[0][:, hs, :], ALU.subtract).then_inc(s_h1, 1)

            def graph_phase(b, at, ph):
                if ph == at["mask"]:
                    graph_inputs(b)
                if ph == at["bias2"]:
                    graph_bias(b)
                if ph == at["h1_low0"]:
                    graph_h1_low(b, 0)
                if ph == at["h1_low1"]:
                    graph_h1_low(b, 1)

            def hidden_low(i, u):
                pool.wait_ge(s_hh, UNITS * i + u + 1)
                nc.gpsimd.tensor_tensor(hhs[1][:, u % 2, :], hb[:, u % 2, :], hhs[0][:, u % 2, :],
                                        ALU.subtract).then_inc(s_hl, 1)

            def graph_only(b, p, par, router=True):
                for ph in range(PHASES):
                    graph_phase(b, POOL_FIRST, ph)
                    if not router and ph in CHUNKS_FIRST:
                        chunk_low(0, CHUNKS_FIRST.index(ph), 0, 0)

            def ffn(base, p, par, graph=True, router=True, ahead=True, first=False, last=False):
                i = base + p
                half = UNITS // 2
                for u in range(UNITS):
                    if graph:
                        graph_phase(i + SB_B, POOL_AT, 3 * u)
                    if u == LAG:
                        pool.wait_ge(s_dn, UNITS * i + CREDIT)
                    if LAG <= u < LAG + NW:
                        chunk_low(1, u - LAG, i, 0)
                    hidden_low(i, u)
                    if u == half + 2:
                        pool.wait_ge(s_dn, UNITS * i + half + CREDIT)
                    if half + 2 <= u < half + 2 + NW and not last:
                        chunk_low(0, u - half - 2, i, 1)
                    if graph:
                        graph_phase(i + SB_B, POOL_AT, 3 * u + 1)
                        graph_phase(i + SB_B, POOL_AT, 3 * u + 2)

            pool.wait_ge(s_gwh, 2)
            nc.gpsimd.tensor_tensor(flat(W1s[1]), stage[:, 0, :], flat(W1s[0]), ALU.subtract)
            nc.gpsimd.tensor_tensor(W2s[1][:, :, 0:D], fold(stage[:, 1, :], KF), W2s[0][:, :, 0:D],
                                    ALU.subtract).then_inc(s_gwl, 1)
            pool.wait_ge(s_av, 16 * 4)
            for n in range(2):
                nc.gpsimd.tensor_tensor(w2_products(n), fold(stage[:, 1, :], KF),
                                        e2[:, 0, n, :].unsqueeze(1).broadcast_to([P, KF, D]), ALU.mult).then_inc(s_v2p, 1)
            pool.wait_ge(s_cin, 16 * 3)
            run_iterations(pool, graph_only, ffn)

        @block.scalar
        def _(act):
            def nT_high(b):
                act.wait_ge(s_T1, b + 1)
                act.wait_ge(s_A2, START + b)
                nc.scalar.activation(flat(nTs[0]), pA[:, :], ACT.Copy).then_inc(s_nTh, 1)

            def mask_bias(b):
                act.wait_ge(s_MT, START + b + 1)
                act.wait_ge(s_max, START + 3 * b)
                nc.scalar.activation(flat(mbias), maskT, ACT.Copy, bias=-MASKED, scale=MASKED).then_inc(s_mb, 1)

            def rows_copy(b):
                act.wait_ge(s_RW, b + 1)
                act.wait_ge(s_SB, START + 2 * b)
                nc.scalar.activation(rows_f[:, :], pA[0:2 * H, 0:N], ACT.Copy)
                nc.scalar.activation(rows_s[0][:, :], pA[0:2 * H, 0:N], ACT.Copy).then_inc(s_rwc, 1)

            def features1_high(b, j):
                act.wait_ge(s_X1, 2 * b + j + 1)
                act.wait_ge(s_A1, START + H * b)
                nc.scalar.activation(xls[0][:, j, :], bank_X1[j][:, :], ACT.Copy).then_inc(s_xlh, 1)

            def exps(b, g):
                act.wait_ge(s_max, START + 3 * b + g + 1)
                if g != 1:
                    act.wait_ge(s_PT, START + (H + 1) * b + g)
                for h in range(2 if g < 2 else 1):
                    if g > 0:
                        act.wait_ge(s_larger, HEADS * b + 2 * g - 1 + h)
                    for j in range(NJ):
                        k = slot(g, h)
                        nc.scalar.activation(e1[:, k, j, :], scores(g)[:, h, j, :], ACT.Exp, bias=bi1[:, j, k:k + 1])
                        last = nc.scalar.activation(e2[:, h, j, :], scores(g)[:, h, j, :], ACT.Exp, bias=bi2[:, j, k:k + 1],
                                                    scale=NEG_SLOPE)
                    last.then_inc(s_exp, 1)

            def probs_high(b, h):
                act.wait_ge(s_PT, START + (H + 1) * b + h + 1)
                if h == 0:
                    act.wait_ge(s_A2, START + b)
                else:
                    act.wait_ge(s_A1, START + H * b + max(h - 1, 0))
                nc.scalar.activation(PTs[0][:, h % 2, :, :].rearrange("p j n -> p (j n)"), bank_PT[h][:, :],
                                     ACT.Copy).then_inc(s_PTh, 1)

            def attended_bias(b, g):
                act.wait_ge(s_A1, START + H * b + 2 * g + 2)
                act.wait_ge(s_h1, START + 2 * b)
                if g == 0:
                    act.wait_ge(s_exp, START + HEADS * b + 4)
                for h in range(2):
                    last = nc.scalar.activation(z[:, 2 * g + h, :], bank_A1[g][:, h * N:(h + 1) * N], ACT.Identity,
                                                bias=b1T[:, 2 * g + h:2 * g + h + 1])
                last.then_inc(s_z, 1)

            def elu_exp(b, g):
                act.wait_ge(s_zn, 2 * b + g + 1)
                nc.scalar.activation(xn2[:, :, :], xn2[:, :, :], ACT.Exp).then_inc(s_ze, 1)

            def h1_high(b, g):
                act.wait_ge(s_zf, 2 * b + g + 1)
                act.wait_ge(s_X2, START + 2 * b)
                nc.scalar.activation(h1s[0][:, 2 * g:2 * g + 2, :], z[:, 2 * g:2 * g + 2, :], ACT.Copy).then_inc(s_h1h, 1)

            def features2_high(b, j):
                act.wait_ge(s_X2, START + 2 * b + j + 1)
                nc.scalar.activation(nTs[0][:, j, :], bank_X2[j][:, 0:D], ACT.Copy).then_inc(s_x2h, 1)

            def ffn_x_high(b, p, par):
                act.wait_ge(s_T2, b + 1)
                nc.scalar.activation(xTs[0][:, :, bass.ds(p * N + par * SB_T, N)], fold(pB), ACT.Copy).then_inc(s_fTh, 1)

            def router_rows(b):
                act.wait_ge(s_RT, b + 1)
                nc.scalar.activation(lrows[:, :], pB[0:E, 0:N], ACT.Copy).then_inc(s_lr, 1)

            def gap_exp(b):
                act.wait_ge(s_gap, b + 1)
                nc.scalar.activation(eg[:, :], gap[:, :], ACT.Exp).then_inc(s_eg, 1)

            def router_phase(b, at, ph):
                if ph == at["RT_rows"]:
                    router_rows(b)
                if ph == at["gap_exp"]:
                    gap_exp(b)

            def graph_phase(b, p, par, at, ph):
                if ph == at["T1_high"]:
                    nT_high(b)
                if ph == at["mask_bias"]:
                    mask_bias(b)
                if ph == at["rows"]:
                    rows_copy(b)
                if ph == at["X1_high0"]:
                    features1_high(b, 0)
                if ph == at["X1_high1"]:
                    features1_high(b, 1)
                if ph == at["exp0"]:
                    exps(b, 0)
                if ph == at["PT_high0"]:
                    probs_high(b, 0)
                if ph == at["PT_high1"]:
                    probs_high(b, 1)
                if ph == at["exp1"]:
                    exps(b, 1)
                if ph == at["bias0"]:
                    attended_bias(b, 0)
                if ph == at["elu_exp0"]:
                    elu_exp(b, 0)
                if ph == at["PT_high2"]:
                    probs_high(b, 2)
                if ph == at["PT_high3"]:
                    probs_high(b, 3)
                if ph == at["bias1"]:
                    attended_bias(b, 1)
                if ph == at["elu_exp1"]:
                    elu_exp(b, 1)
                if ph == at["h1_high0"]:
                    h1_high(b, 0)
                if ph == at["h1_high1"]:
                    h1_high(b, 1)
                if ph == at["X2_high0"]:
                    features2_high(b, 0)
                if ph == at["X2_high1"]:
                    features2_high(b, 1)
                if ph == at["exp2"]:
                    exps(b, 2)
                if ph == at["PT_high4"]:
                    probs_high(b, H)
                if ph == at["T2_high"]:
                    ffn_x_high(b, p, par)

            def chunk_high(el, c, i, ahead):
                k = NW * el + c
                act.wait_ge(s_wst[k % 2], 8 * NWI * (i + ahead) + 16 * (k // 2) + 16)
                nc.scalar.activation(flat((we1, we3, we2)[c][el][0]), stage[:, k % 2, :], ACT.Copy).then_inc(s_wh, 1)

            def gate_tanh(i, u):
                act.wait_ge(s_g, UNITS * i + u + 1)
                act.wait_ge(s_hl, UNITS * i + u + 1)
                nc.scalar.activation(hb[:, u % 2, :], pG[u % 2][:, :], ACT.Tanh, scale=0.5).then_inc(s_th, 1)

            def hidden_high(i, u):
                act.wait_ge(s_h, UNITS * i + u + 1 + CREDIT)
                act.wait_ge(s_dn, UNITS * i + u + 1)
                nc.scalar.activation(hhs[0][:, u % 2, :], hb[:, u % 2, :], ACT.Copy).then_inc(s_hh, 1)

            def graph_only(b, p, par, router=True):
                for ph in range(PHASES):
                    if router:
                        router_phase(b - 1, ACT_FIRST, ph)
                    graph_phase(b, p, par, ACT_FIRST, ph)
                    if not router and ph in CHUNKS_FIRST:
                        chunk_high(0, CHUNKS_FIRST.index(ph), 0, 0)

            def ffn(base, p, par, graph=True, router=True, ahead=True, first=False, last=False):
                i = base + p
                half = UNITS // 2
                for u in range(UNITS):
                    gate_tanh(i, u)
                    if router:
                        router_phase(i + SB_B - 1, ACT_AT, 3 * u)
                    if graph:
                        graph_phase(i + SB_B, p, 1 - par, ACT_AT, 3 * u)
                    if router:
                        router_phase(i + SB_B - 1, ACT_AT, 3 * u + 1)
                    if graph:
                        graph_phase(i + SB_B, p, 1 - par, ACT_AT, 3 * u + 1)
                    hidden_high(i, u)
                    if u == LAG:
                        act.wait_ge(s_dn, UNITS * i + CREDIT)
                    if LAG <= u < LAG + NW:
                        chunk_high(1, u - LAG, i, 0)
                    if u == half + 2:
                        act.wait_ge(s_dn, UNITS * i + half + CREDIT)
                    if half + 2 <= u < half + 2 + NW and not last:
                        chunk_high(0, u - half - 2, i, 1)
                    if router:
                        router_phase(i + SB_B - 1, ACT_AT, 3 * u + 2)
                    if graph:
                        graph_phase(i + SB_B, p, 1 - par, ACT_AT, 3 * u + 2)

            act.sem_inc(s_exp, START)
            act.sem_inc(s_lr, START)
            act.wait_ge(s_w12, 32)
            nc.scalar.activation(flat(W1s[0]), stage[:, 0, :], ACT.Copy).then_inc(s_gwh, 1)
            nc.scalar.activation(W2s[0][:, :, 0:D], fold(stage[:, 1, :], KF), ACT.Copy).then_inc(s_gwh, 1)
            act.wait_ge(s_cin, 16 * 3)
            run_iterations(act, graph_only, ffn)

        @block.vector
        def _(dve):
            prepared = [0]

            def prep(ins):
                prepared[0] += 1
                ins.then_inc(s_prep, 1)
                dve.wait_ge(s_prep, prepared[0])

            def set_up():
                dve.wait_ge(s_w12, 32)
                dve.wait_ge(s_cz, 1)
                dve.wait_ge(s_av, 16 * 4)
                tmp = sc[:, :, :, :].rearrange("p a j n -> p (a j n)")
                for k in range(KD):
                    for n in range(2):
                        prep(nc.vector.tensor_tensor(tmp[:, 0:HF], stage[:, 0, k * HF:(k + 1) * HF], hb[:, n, :], ALU.mult))
                        prep(nc.vector.tensor_reduce(z[:, KD + k, P + n * H:P + (n + 1) * H],
                                                     tmp[:, 0:HF].rearrange("p (h f) -> p h f", h=H), AX_X, ALU.add))
                dve.wait_ge(s_cin, 16 * 3)
                nc.vector.tensor_copy(rws[0][:, :, :], z[:, 0:KD, P:2 * P])
                prep(nc.vector.tensor_copy(v1s[0][:, :, :], z[:, KD:2 * KD, P:2 * P]))
                nc.vector.tensor_tensor(rws[1][:, :, :], z[:, 0:KD, P:2 * P], rws[0][:, :, :], ALU.subtract)
                nc.vector.tensor_tensor(v1s[1][:, :, :], z[:, KD:2 * KD, P:2 * P], v1s[0][:, :, :], ALU.subtract)
                for n in range(2):
                    dve.wait_ge(s_v2p, n + 1)
                    last = nc.vector.tensor_reduce(v2f[:, :, n], w2_products(n), AX_X, ALU.add)
                prep(last)
                prep(nc.vector.tensor_copy(W2s[0][:, :, D:W2N], v2f[:, :, :]))
                dve.wait_ge(s_gwl, 1)
                nc.vector.tensor_tensor(W2s[1][:, :, D:W2N], v2f[:, :, :], W2s[0][:, :, D:W2N],
                                        ALU.subtract).then_inc(s_prepd, 1)

            dve.sem_inc(s_a, CREDIT)
            dve.sem_inc(s_h, CREDIT)
            for s_ in (s_max, s_lg, s_y):
                dve.sem_inc(s_, START)

            links = [0]
            router_links = [0]

            def link(ins, b):
                links[0] += 1
                ins.then_inc(s_dg, 1)
                dve.wait_ge(s_dg, DVE_LINKS * b + links[0])

            def router_link(ins, b):
                router_links[0] += 1
                ins.then_inc(s_dr, 1)
                dve.wait_ge(s_dr, ROUTER_LINKS * b + router_links[0])

            var_h, root, root_s = (nw[:, k, :] for k in range(3))

            def norm_link(ins, b, which, n):
                ins.then_inc(s_norm, 1)
                dve.wait_ge(s_norm, NORM_LINKS * (2 * b + which) + n)

            def norm_seed(b, which, rows):
                for j in range(NJ):
                    last = nc.vector.bn_stats(st[:, j, :], rows[j])
                last.then_inc(s_norm, 1)
                wait_alone(dve, (s_norm, NORM_LINKS * (2 * b + which) + 1))
                for j in range(NJ):
                    last = nc.vector.bn_aggr(mv[:, j, :], st[:, j, :])
                norm_link(last, b, which, 2)
                norm_link(nc.vector.tensor_scalar(var_h, mv[:, :, 1], LN_EPS, 0.5, ALU.add, ALU.mult), b, which, 3)
                norm_link(nc.vector.tensor_scalar(root_s.bitcast(I32), var_h.bitcast(I32), 1, None,
                                                  ALU.arith_shift_right), b, which, 4)
                nc.vector.tensor_scalar(root.bitcast(I32), root_s.bitcast(I32), -1.0, RSQRT_SEED, ALU.mult,
                                        ALU.add).then_inc(s_norm, 1)

            def norm_root(b, which, rows, xn, done):
                dve.wait_ge(s_norm, NORM_LINKS * (2 * b + which) + 5)
                for n in range(NEWTON_STEPS):
                    for j in range(NJ):
                        last = nc.vector.tensor_scalar(root_s[:, j:j + 1], root[:, j:j + 1], root[:, j:j + 1],
                                                       var_h[:, j:j + 1], ALU.mult, ALU.mult)
                    norm_link(last, b, which, 6 + 2 * n)
                    norm_link(nc.vector.scalar_tensor_tensor(root, root_s, -1.5, root, ALU.add, ALU.mult), b, which, 7 + 2 * n)
                for j in range(NJ):
                    last = nc.vector.tensor_scalar(xn[:, j, :], rows[j], mv[:, j, 0:1], root[:, j:j + 1],
                                                   ALU.subtract, ALU.mult)
                last.then_inc(done, 1)

            def norm1_seed(b):
                dve.wait_ge(s_x, 16 * b + 16)
                norm_seed(b, 0, [xb[:, j, :] for j in range(NJ)])

            def norm1_root(b):
                norm_root(b, 0, [xb[:, j, :] for j in range(NJ)], xn1, s_ln1)

            def norm2_seed(b, p, par):
                wait_alone(dve, (s_x1, b + 1))
                norm_seed(b, 1, [yacc[:, tokens(p, par, j), :] for j in range(NJ)])

            def norm2_root(b, p, par):
                norm_root(b, 1, [yacc[:, tokens(p, par, j), :] for j in range(NJ)], xn2, s_ln2)

            def nT_low(b):
                dve.wait_ge(s_nTh, b + 1)
                nc.vector.tensor_tensor(flat(nTs[1]), pA[:, :], flat(nTs[0]), ALU.subtract).then_inc(s_nT, 1)

            def rows_low(b):
                dve.wait_ge(s_rwc, b + 1)
                nc.vector.tensor_tensor(rows_s[1][:, :], pA[0:2 * H, 0:N], rows_s[0][:, :], ALU.subtract).then_inc(s_rwl, 1)

            def cols_copy(b):
                dve.wait_ge(s_CT, b + 1)
                nc.vector.tensor_copy(flat(cols), pA[:, 0:NJ * 2 * H]).then_inc(s_cols, 1)

            def features1_low(b, j):
                dve.wait_ge(s_xlh, 2 * b + j + 1)
                nc.vector.tensor_tensor(xls[1][:, j, :], bank_X1[j][:, :], xls[0][:, j, :], ALU.subtract).then_inc(s_xll, 1)

            def softmax_max(b, g):
                exps_done = (s_exp, START + HEADS * b + (2 if g == 2 else 0))
                if g == 1:
                    dve.wait_ge(s_h1, START + 2 * b)
                if g < 2:
                    wait_alone(dve, exps_done, (s_SB, START + 2 * b + g + 1), (s_mb, b + 1), (s_cols, b + 1))
                    spread, target, nh = (pA, pB)[g], cols[:, :, H + 2 * g:H + 2 * g + 2], 2
                else:
                    wait_alone(dve, exps_done, (s_B2, b + 1))
                    spread, target, nh = pA, a2c[:, :, 1:2], 1
                for h in range(nh):
                    for j in range(NJ):
                        last = nc.vector.tensor_tensor_reduce(scores(g)[:, h, j, :], spread[:, h * N:(h + 1) * N], mbias[:, j, :],
                                                              1.0, LOWEST, ALU.add, ALU.max, mx[:, j, h:h + 1])
                link(last, b)
                m, mt, at = mm_[:, :, 0:nh], mx[:, :, 0:nh], slot(g, 0)
                link(nc.vector.tensor_tensor(mt, mt, target, ALU.add), b)
                link(nc.vector.scalar_tensor_tensor(m, mt, NEG_SLOPE, mt, ALU.mult, ALU.max), b)
                nc.vector.tensor_tensor(bi1[:, :, at:at + nh], target, m, ALU.subtract)
                nc.vector.scalar_tensor_tensor(bi2[:, :, at:at + nh], target, NEG_SLOPE, m, ALU.mult,
                                               ALU.subtract).then_inc(s_max, 1)

            def softmax_probs(b, g):
                nh = 2 if g < 2 else 1
                for h in range(nh):
                    dve.wait_ge(s_exp, START + HEADS * b + 2 * g + h + 1)
                    for j in range(NJ):
                        e = e1[:, slot(g, h), j, :]
                        last = nc.vector.scalar_tensor_tensor(e, e, 1.0, e2[:, h, j, :], ALU.mult, ALU.max,
                                                              accum_out=sm[:, j, h:h + 1])
                    last.then_inc(s_larger, 1)
                dve.wait_ge(s_larger, HEADS * b + 2 * g + nh)
                if g == 2:
                    nc.vector.reciprocal(rs[:, :, 0:1], sm[:, :, 0:1]).then_inc(s_pn, 1)
                    return
                link(nc.vector.reciprocal(rs[:, :, :], sm[:, :, :]), b)
                for h in range(nh):
                    for j in range(NJ):
                        e = e1[:, slot(g, h), j, :]
                        last = nc.vector.tensor_scalar(e, e, rs[:, j, h:h + 1], None, ALU.mult)
                    last.then_inc(s_pn, 1)

            def probs_low(b, h):
                dve.wait_ge(s_PTh, (H + 1) * b + h + 1)
                dst = (pt[:, h % 2, :, :].rearrange("p j n -> p (j n)") for pt in PTs)
                hi, lo = dst
                nc.vector.tensor_tensor(lo, bank_PT[h][:, :], hi, ALU.subtract).then_inc(s_PTl, 1)

            def elu_negative(b, g):
                dve.wait_ge(s_z, 2 * b + g + 1)
                if g == 1:
                    dve.wait_ge(s_zf, 2 * b + 1)
                zs, ts = z[:, 2 * g:2 * g + 2, :], xn2[:, :, :]
                nc.vector.tensor_scalar(ts, zs, 0.0, None, ALU.min).then_inc(s_zn, 1)
                dve.wait_ge(s_zn, 2 * b + g + 1)
                link(nc.vector.tensor_scalar(zs, zs, 0.0, None, ALU.max), b)

            def elu_sum(b, g):
                dve.wait_ge(s_ze, 2 * b + g + 1)
                zs, ts = z[:, 2 * g:2 * g + 2, :], xn2[:, :, :]
                nc.vector.scalar_tensor_tensor(zs.rearrange("p a b -> p (a b)"), ts.rearrange("p a b -> p (a b)"), -1.0,
                                               zs.rearrange("p a b -> p (a b)"), ALU.add, ALU.add).then_inc(s_zf, 1)

            def features2_low(b, j):
                dve.wait_ge(s_x2h, 2 * b + j + 1)
                nc.vector.tensor_copy(a2c[:, j, :], bank_X2[j][:, D:W2N])
                nc.vector.tensor_tensor(nTs[1][:, j, :], bank_X2[j][:, 0:D], nTs[0][:, j, :], ALU.subtract).then_inc(s_x2l, 1)

            def source2(b):
                dve.wait_ge(s_x2l, 2 * b + 2)
                src = a2c[:, :, 0:1].broadcast_to([P, NJ, P])
                link(nc.vector.tensor_copy(a2s[0][:, :, :], src), b)
                nc.vector.tensor_tensor(a2s[1][:, :, :], src, a2s[0][:, :, :], ALU.subtract).then_inc(s_a2, 1)

            def tokens(p, par, j):
                return bass.ds(p * NJ + par * SB_B * NJ + j, 1)

            def residual1(b, p, par, base):
                dve.wait_ge(s_A2, START + b + 1)
                dve.wait_ge(s_xb2, b + 1)
                if base is not None:
                    dve.wait_ge(s_out, START + base * (16 * NBLK // SB_B))
                for j in range(NJ):
                    last = nc.vector.scalar_tensor_tensor(yacc[:, tokens(p, par, j), :], pA[:, j * D:(j + 1) * D],
                                                          rs[:, j, 0:1], xb[:, j, :], ALU.mult, ALU.add)
                last.then_inc(s_x1, 1)

            def ffn_x_low(b, p, par):
                dve.wait_ge(s_fTh, b + 1)
                at = bass.ds(p * N + par * SB_T, N)
                nc.vector.tensor_tensor(xTs[1][:, :, at], fold(pB), xTs[0][:, :, at], ALU.subtract).then_inc(s_fT, 1)

            def router_top(b):
                dve.wait_ge(s_LC, b + 1)
                nc.vector.tensor_copy(flat(lg), pB[:, 0:NJ * E]).then_inc(s_lg, 1)
                wait_alone(dve, (s_lg, START + b + 1))
                for j in range(NJ):
                    last = nc.vector.max(top[:, j, :], lg[:, j, :])
                router_link(last, b)
                nc.vector.tensor_tensor(gap[:, :], top[:, :, 1], top[:, :, 0], ALU.subtract).then_inc(s_gap, 1)
                for j in range(NJ):
                    last = nc.vector.max_index(topi[:, j, :], top[:, j, :], lg[:, j, :])
                router_link(last, b)
                router_link(nc.vector.tensor_copy(flat(topf), flat(topi)), b)

            def router_weights(b):
                dve.wait_ge(s_eg, b + 1)
                s, w0, w1_ = (wts[:, k, :] for k in range(3))
                router_link(nc.vector.tensor_scalar(s, eg[:, :], 2.0, 2.0, ALU.mult, ALU.add), b)
                router_link(nc.vector.reciprocal(w0, s), b)
                router_link(nc.vector.tensor_tensor(w1_, eg[:, :], w0, ALU.mult), b)
                for j in range(NJ):
                    for k, w in enumerate((w0, w1_)):
                        last = nc.vector.tensor_scalar(oh[:, k, j, :], expert_id[:, :], topf[:, j, k:k + 1], w[:, j:j + 1],
                                                       ALU.is_equal, ALU.mult)
                router_link(last, b)
                nc.vector.tensor_tensor(comb[:, bass.ds(b % (2 * SB_B) * NJ, NJ), :], oh[:, 0, :, :], oh[:, 1, :, :],
                                        ALU.add).then_inc(s_comb, 1)

            def router_phase(b, at, ph):
                if ph == at["top"]:
                    router_top(b)
                if ph == at["comb"]:
                    router_weights(b)

            def graph_phase(b, p, par, base, at, ph, ahead=True):
                if ph == at["T1_low"]:
                    nT_low(b)
                if ph == at["rows_low"]:
                    rows_low(b)
                if ph == at["X1_low0"]:
                    features1_low(b, 0)
                if ph == at["cols"]:
                    cols_copy(b)
                if ph == at["X1_low1"]:
                    features1_low(b, 1)
                if ph == at["max0"]:
                    softmax_max(b, 0)
                if ph == at["prob0"]:
                    softmax_probs(b, 0)
                if ph == at["max1"]:
                    softmax_max(b, 1)
                if ph == at["PT_low0"]:
                    probs_low(b, 0)
                if ph == at["PT_low1"]:
                    probs_low(b, 1)
                if ph == at["elu_neg0"]:
                    elu_negative(b, 0)
                if ph == at["prob1"]:
                    softmax_probs(b, 1)
                if ph == at["PT_low2"]:
                    probs_low(b, 2)
                if ph == at["elu_sum0"]:
                    elu_sum(b, 0)
                if ph == at["PT_low3"]:
                    probs_low(b, 3)
                if ph == at["elu_neg1"]:
                    elu_negative(b, 1)
                if ph == at["elu_sum1"]:
                    elu_sum(b, 1)
                if ph == at["X2_low0"]:
                    features2_low(b, 0)
                if ph == at["X2_low1"]:
                    features2_low(b, 1)
                if ph == at["source2"]:
                    source2(b)
                if ph == at["max2"]:
                    softmax_max(b, 2)
                if ph == at["prob2"]:
                    softmax_probs(b, 2)
                if ph == at["PT_low4"]:
                    probs_low(b, H)
                if ph == at["x1"]:
                    residual1(b, p, par, base)
                if ph == at["norm2"]:
                    norm2_seed(b, p, par)
                if ph == at["root2"]:
                    norm2_root(b, p, par)
                if ph == at["T2_low"]:
                    ffn_x_low(b, p, par)
                if ph == at["norm1_next"] and ahead:
                    norm1_seed(b + 1)
                if ph == at["root1_next"] and ahead:
                    norm1_root(b + 1)

            def pair_weights(i, base, p, par):
                dve.wait_ge(s_comb, base + SB_B)
                dve.wait_ge(s_y, START + GROUPS * i)
                nc.vector.tensor_copy(cw[:, :, :], comb[:, par * SB_B * NJ:(par + 1) * SB_B * NJ,
                                                        bass.ds(p * EI, EI)]).then_inc(s_cw, 1)
                dve.wait_ge(s_cw, i + 1)
                dve.wait_ge(s_x1, base + SB_B)

            def gate_product(i, u):
                dve.wait_ge(s_th, UNITS * i + u + 1)
                hu = hb[:, u % 2, :]
                nc.vector.scalar_tensor_tensor(hu, hu, 1.0, pG[u % 2][:, :], ALU.add, ALU.mult).then_inc(s_a, 1)

            def hidden(i, u):
                dve.wait_ge(s_u, UNITS * i + u + 1)
                dve.wait_ge(s_a, UNITS * i + u + 1 + CREDIT)
                hu = hb[:, u % 2, :]
                nc.vector.tensor_tensor(hu, hu, pU[u % 2][:, :], ALU.mult).then_inc(s_h, 1)

            def add_y(i, g, half):
                el, blk = divmod(g, NBLK)
                dve.wait_ge(s_dn, UNITS * i + (g + 1) * FT + CREDIT)
                dve.wait_ge(s_y, START + GROUPS * i + g)
                for tt in range(TT):
                    tile = blk * TT + tt
                    acc = yacc[:, bass.ds(half * (SB_B * NJ) + tile, 1), :]
                    last = nc.vector.scalar_tensor_tensor(acc, pY[tt // 2][:, tt % 2, :], cw[:, tile, el:el + 1], acc,
                                                          ALU.mult, ALU.add)
                last.then_inc(s_y, 1)

            def graph_only(b, p, par, router=True):
                links[0] = router_links[0] = 0
                for ph in range(PHASES):
                    if router:
                        router_phase(b - 1, DVE_FIRST, ph)
                    graph_phase(b, p, par, None, DVE_FIRST, ph)
                assert links[0] == DVE_LINKS, links[0]

            def ffn(base, p, par, graph=True, router=True, ahead=True, first=False, last=False):
                i = base + p
                links[0] = router_links[0] = 0
                for u in range(UNITS):
                    gate_product(i, u)
                    if router:
                        router_phase(i + SB_B - 1, DVE_AT, 3 * u)
                    if graph:
                        graph_phase(i + SB_B, p, 1 - par, base, DVE_AT, 3 * u, ahead)
                    if router:
                        router_phase(i + SB_B - 1, DVE_AT, 3 * u + 1)
                    if graph:
                        graph_phase(i + SB_B, p, 1 - par, base, DVE_AT, 3 * u + 1, ahead)
                    hidden(i, u)
                    if router:
                        router_phase(i + SB_B - 1, DVE_AT, 3 * u + 2)
                    if graph:
                        graph_phase(i + SB_B, p, 1 - par, base, DVE_AT, 3 * u + 2, ahead)
                    if u == LAG - 1 and not first:
                        add_y(i - 1, GROUPS - 1, (i - 1) // SB_B % 2)
                    elif u % FT == LAG - 1 and u >= FT:
                        if u == FT + LAG - 1:
                            pair_weights(i, base, p, par)
                        add_y(i, u // FT - 1, par)
                if last:
                    add_y(i, GROUPS - 1, par)

            norm1_seed(0)
            norm1_root(0)
            set_up()
            run_iterations(dve, graph_only, ffn)

        @block.tensor
        def _(pe):
            def pairs(a, b):
                return ((a[0], b[0]), (a[1], b[0]), (a[0], b[1]))

            def product(dst, terms):
                for n, (lhsT, rhs) in enumerate(terms):
                    last = nc.tensor.matmul(dst, lhsT, rhs, start=(n == 0), stop=(n == len(terms) - 1))
                return last

            def transpose_norm(b, xn, bank, done):
                for k in range(KD):
                    for j in range(NJ):
                        last = nc.tensor.transpose(bank[:, k * N + j * P:k * N + (j + 1) * P], xn[:, j, k * P:(k + 1) * P],
                                                   ident[:, :])
                last.then_inc(done, 1)

            def T1(b):
                pe.wait_ge(s_ln1, b + 1)
                transpose_norm(b, xn1, pA, s_T1)

            def MT(b):
                pe.wait_ge(s_mask, b + 1)
                pe.wait_ge(s_lg, START + b)
                for jt in range(NJ):
                    for js in range(NJ):
                        last = nc.tensor.transpose(maskT[:, jt * N + js * P:jt * N + (js + 1) * P],
                                                   mask[:, js, jt * P:(jt + 1) * P], ident_b[:, :])
                last.then_inc(s_MT, 1)

            def RW(b):
                pe.wait_ge(s_nT, b + 1)
                product(pA[:, 0:N], [(v[:, k, :], n[:, k, :]) for k in range(KD) for v, n in pairs(v1s, nTs)]).then_inc(s_RW, 1)

            def X1(b, j):
                pe.wait_ge(s_max, START + 3 * b + j + 1)
                product(bank_X1[j][:, :], [(n[:, k, j * P:(j + 1) * P], w[:, k, :]) for k in range(KD)
                                   for n, w in pairs(nTs, W1s)]).then_inc(s_X1, 1)

            def CT(b):
                wait_alone(pe, (s_rwl, b + 1))
                for j in range(NJ):
                    last = nc.tensor.transpose(pA[:, j * 2 * H:(j + 1) * 2 * H], rows_f[:, j * P:(j + 1) * P],
                                               ident[0:2 * H, 0:2 * H])
                last.then_inc(s_CT, 1)

            def SB(b, g):
                if g == 0:
                    pe.wait_ge(s_cols, b + 1)
                else:
                    pe.wait_ge(s_mb, b + 1)
                for h in range(2):
                    last = product((pA, pB)[g][:, h * N:(h + 1) * N],
                                   [(head_row[:, 2 * g + h, :], r[:, :]) for r in rows_s])
                last.then_inc(s_SB, 1)

            def PT(b, h):
                pe.wait_ge(s_pn, HEADS * b + h + 1)
                if h == 0:
                    pe.wait_ge(s_xll, 2 * b + 1)
                elif h == 1:
                    pe.wait_ge(s_xll, 2 * b + 2)
                elif h in (2, 3):
                    if h == 2:
                        pe.wait_ge(s_PTl, 5 * b + 2)
                    else:
                        pe.wait_ge(s_z, 2 * b + 1)
                else:
                    pe.wait_ge(s_x2l, 2 * b + 2)
                for js in range(NJ):
                    for jt in range(NJ):
                        last = nc.tensor.transpose(bank_PT[h][:, js * N + jt * P:js * N + (jt + 1) * P],
                                                   e1[:, h % H, jt, js * P:(js + 1) * P], ident[:, :])
                last.then_inc(s_PT, 1)

            def A1(b, h):
                pe.wait_ge(s_PTl, 5 * b + h + 1)
                if h == 0:
                    pe.wait_ge(s_xll, 2 * b + 2)
                if h == 2:
                    pe.wait_ge(s_PTl, 5 * b + 3)
                product(bank_A1[h // 2][:, (h % 2) * N:(h % 2 + 1) * N],
                        [(xl[:, j, h * P:(h + 1) * P], pt[:, h % 2, j, :]) for j in range(NJ)
                         for xl, pt in pairs(xls, PTs)]).then_inc(s_A1, 1)

            def X2_part(b, j, k0, k1):
                terms = [(h[:, k, j * P:(j + 1) * P], w[:, k, :]) for k in range(k0, k1) for h, w in pairs(h1s, W2s)]
                for n, (h, w) in enumerate(terms):
                    last = nc.tensor.matmul(bank_X2[j][:, 0:W2N], h, w, start=(k0 == 0 and n == 0),
                                            stop=(k1 == KF and n == len(terms) - 1))
                return last

            def X2_head(b):
                pe.wait_ge(s_h1, START + 2 * b + 1)
                pe.wait_ge(s_z, 2 * b + 2)
                for j in range(NJ):
                    X2_part(b, j, 0, KF // 2)

            def X2(b, j):
                pe.wait_ge(s_h1, START + 2 * b + 2)
                X2_part(b, j, KF // 2, KF).then_inc(s_X2, 1)

            def B2(b):
                pe.wait_ge(s_a2, b + 1)
                for j in range(NJ):
                    last = product(pA[:, j * P:(j + 1) * P], [(a[:, j, :], ident_r[:, :]) for a in a2s])
                last.then_inc(s_B2, 1)

            def A2(b):
                pe.wait_ge(s_PTl, 5 * b + 5)
                pe.wait_ge(s_max, START + 3 * b + 3)
                for jt in range(NJ):
                    last = product(pA[:, jt * D:(jt + 1) * D], [(pt[:, 0, js, jt * P:(jt + 1) * P], xl[:, js, :])
                                                                for js in range(NJ) for pt, xl in pairs(PTs, nTs)])
                last.then_inc(s_A2, 1)

            def T2(b):
                pe.wait_ge(s_ln2, b + 1)
                transpose_norm(b, xn2, pB, s_T2)

            def RT(b):
                pe.wait_ge(s_fT, b + 1)
                at = bass.ds(b % (2 * SB_B) * N, N)
                product(pB[:, 0:N], [(r[:, k, :], xt[:, k, at]) for k in range(KD) for r, xt in pairs(rws, xTs)]).then_inc(s_RT, 1)

            def LC(b):
                wait_alone(pe, (s_lr, START + b + 1))
                for j in range(NJ):
                    last = nc.tensor.transpose(pB[:, j * E:(j + 1) * E], lrows[:, j * P:(j + 1) * P], ident[0:E, 0:E])
                last.then_inc(s_LC, 1)

            def router_phase(b, at, ph):
                if ph == at["RT"]:
                    RT(b)
                if ph == at["LC"]:
                    LC(b)

            def graph_phase(b, p, par, at, ph):
                if ph == at["T1"]:
                    T1(b)
                if ph == at["MT"]:
                    MT(b)
                if ph == at["RW"]:
                    RW(b)
                if ph == at["X1_0"]:
                    X1(b, 0)
                if ph == at["CT"]:
                    CT(b)
                if ph == at["X1_1"]:
                    X1(b, 1)
                if ph == at["SB0"]:
                    SB(b, 0)
                if ph == at["SB1"]:
                    SB(b, 1)
                if ph == at["PT0"]:
                    PT(b, 0)
                if ph == at["PT1"]:
                    PT(b, 1)
                if ph == at["A1_0"]:
                    A1(b, 0)
                if ph == at["A1_1"]:
                    A1(b, 1)
                if ph == at["PT2"]:
                    PT(b, 2)
                if ph == at["PT3"]:
                    PT(b, 3)
                if ph == at["A1_2"]:
                    A1(b, 2)
                if ph == at["A1_3"]:
                    A1(b, 3)
                if ph == at["X2_head"]:
                    X2_head(b)
                if ph == at["X2_0"]:
                    X2(b, 0)
                if ph == at["X2_1"]:
                    X2(b, 1)
                if ph == at["B2"]:
                    B2(b)
                if ph == at["PT4"]:
                    PT(b, H)
                if ph == at["A2"]:
                    A2(b)
                if ph == at["T2"]:
                    T2(b)

            def gate(i, u, par):
                if u % (NBLK * FT) == 0:
                    pe.wait_ge(s_wl, NWI * i + NW * (u // (NBLK * FT)) + 1)
                pe.wait_ge(s_a, UNITS * i + u + 1)
                expand(we1, pG, u, par).then_inc(s_g, 1)

            def up(i, u, par):
                if u % (NBLK * FT) == 0:
                    pe.wait_ge(s_wl, NWI * i + NW * (u // (NBLK * FT)) + 2)
                pe.wait_ge(s_h, UNITS * i + u + 1)
                expand(we3, pU, u, par).then_inc(s_u, 1)

            def expand(we, bank, u, par):
                el, blk, ft = u // (NBLK * FT), u // FT % NBLK, u % FT
                at = slice(par * SB_T + blk * BLK, par * SB_T + (blk + 1) * BLK)
                return product(bank[u % 2][:, :], [(w[:, k, ft * P:(ft + 1) * P], xt[:, k, at]) for k in range(KD)
                                                   for w, xt in pairs(we[el], xTs)])

            def down(i, u):
                el, ft = u // (NBLK * FT), u % FT
                if u % (NBLK * FT) == 0:
                    pe.wait_ge(s_wl, NWI * i + NW * el + NW)
                if ft == 0:
                    pe.wait_ge(s_y, START + GROUPS * i + u // FT)
                pe.wait_ge(s_hl, UNITS * i + u + 1 + CREDIT)
                for tt in range(TT):
                    ts = slice(tt * P, (tt + 1) * P)
                    for n, (h, w) in enumerate(pairs(hhs, we2[el])):
                        last = nc.tensor.matmul(pY[tt // 2][:, tt % 2, :], h[:, u % 2, ts], w[:, ft, :],
                                                start=(ft == 0 and n == 0 and tt % 2 == 0),
                                                stop=(ft == FT - 1 and n == 2), skip_group_check=True)
                last.then_inc(s_dn, 1)

            def graph_only(b, p, par, router=True):
                for ph in range(PHASES):
                    if router:
                        router_phase(b - 1, PE_FIRST, ph)
                    if not router and ph == PE_FIRST["RW"]:
                        pe.wait_ge(s_prepd, 1)
                    graph_phase(b, p, par, PE_FIRST, ph)

            def ffn(base, p, par, graph=True, router=True, ahead=True, first=False, last=False):
                i = base + p
                pe.wait_ge(s_fT, base + SB_B)
                for u in range(UNITS):
                    gate(i, u, par)
                    if router:
                        router_phase(i + SB_B - 1, PE_AT, 3 * u)
                    if graph:
                        graph_phase(i + SB_B, p, 1 - par, PE_AT, 3 * u)
                    up(i, u, par)
                    if router:
                        router_phase(i + SB_B - 1, PE_AT, 3 * u + 1)
                    if graph:
                        graph_phase(i + SB_B, p, 1 - par, PE_AT, 3 * u + 1)
                    if u >= LAG:
                        down(i, u - LAG)
                    elif not first:
                        down(i - 1, UNITS + u - LAG)
                    if router:
                        router_phase(i + SB_B - 1, PE_AT, 3 * u + 2)
                    if graph:
                        graph_phase(i + SB_B, p, 1 - par, PE_AT, 3 * u + 2)
                if last:
                    for u in range(UNITS - LAG, UNITS):
                        down(i, u)

            pe.sem_inc(s_dn, CREDIT)
            for s_ in (s_MT, s_SB, s_A1, s_A2, s_PT, s_X2):
                pe.sem_inc(s_, START)
            pe.wait_ge(s_cr, 1)
            run_iterations(pe, graph_only, ffn)


_INS = ['x', 'adj', 'L0_gnn_W1', 'L0_gnn_att_src1', 'L0_gnn_att_dst1', 'L0_gnn_b1', 'L0_gnn_W2', 'L0_gnn_att_src2',
        'L0_gnn_att_dst2', 'L0_gnn_b2', 'L0_ffn_router_w', 'L0_ffn_w1', 'L0_ffn_w2', 'L0_ffn_w3']
_OUTS = [((32, 256, 256), 'float32')]


def kernel(**inputs):
    import numpy as _np
    import concourse.bacc as _bacc
    from concourse import mybir as _mybir
    from concourse.bass_utils import run_bass_kernel_spmd as _run

    nc = _bacc.Bacc("TRN2", target_bir_lowering=False, num_devices=1)
    arrays, args = {}, []
    for name in _INS:
        a = _np.ascontiguousarray(inputs[name])
        arrays[f"in_{name}_dram"] = a
        args.append(nc.dram_tensor(f"in_{name}_dram", a.shape, _mybir.dt.from_np(a.dtype), kind="ExternalInput").ap())
    for i, (shape, dtype) in enumerate(_OUTS):
        dt = _mybir.dt.from_np(_np.dtype(dtype))
        args.append(nc.dram_tensor(f"out_{i}_dram", shape, dt, kind="ExternalOutput").ap())
    gat_moe_kernel(nc, *args)
    r = _run(nc, [arrays], core_ids=[0])
    got = tuple(r.results[0][f"out_{i}_dram"] for i in range(len(_OUTS)))
    return got[0]
```
